# Optimizing a Trainium2 kernel written in Bass

```python
import numpy as np
import jax
import jax.numpy as jnp

def _softmax(x, axis=-1):
    return jax.nn.softmax(x, axis=axis)

def _gelu(x):
    return jax.nn.gelu(x, approximate=True)

def _silu(x):
    return jax.nn.silu(x)

def _sigmoid(x):
    return jax.nn.sigmoid(x)

def _layernorm(x, axis=-1, eps=1e-05):
    m = jnp.mean(x, axis=axis, keepdims=True)
    v = jnp.var(x, axis=axis, keepdims=True)
    return (x - m) / jnp.sqrt(v + eps)

def _scatter_add(tgt, idx, src, axis=0):
    return tgt.at[idx].add(src)

def _segment_sum(src, seg, n):
    return jax.ops.segment_sum(src, seg, n)
kernel_name = 'mk_xattn_ffn_d1_seqx_r4_90878f'

def setup_inputs(seed: int=0):
    np.random.seed(seed)
    _w = jnp.asarray

    def _rec_inputs():
        import jax
        import jax.numpy as jnp
        _rk = jax.random.key(seed)
        x = -0.0002928 + 1 * jax.random.normal(jax.random.fold_in(_rk, 1), (32, 112, 256), jnp.float32)
        _lenS = 112 - jax.random.randint(jax.random.fold_in(_rk, 7), (32,), 0, max(1, 112 // 4) + 1, jnp.int32)
        _lenS2 = 375 - jax.random.randint(jax.random.fold_in(_rk, 8), (32,), 0, max(1, 375 // 4) + 1, jnp.int32)
        _ctx_768P = jax.random.normal(jax.random.fold_in(_rk, 11), (32, 16, 192), jnp.float32)
        _ctx_768c = jax.random.dirichlet(jax.random.fold_in(_rk, 511), 0.3 * jnp.ones((16,), jnp.float32), (32, 375))
        _ctx_768t = jnp.einsum('bsk,bkd->bsd', _ctx_768c, _ctx_768P)
        _ctx_768t = _ctx_768t * jax.lax.rsqrt(jnp.mean(jnp.square(_ctx_768t)) + 1e-12) * 0.953939
        ctx_768 = 2.09791e-05 + 1.00001 * (_ctx_768t + 0.3 * jax.random.normal(jax.random.fold_in(_rk, 611), (32, 375, 192), jnp.float32))
        return (x, ctx_768)
    x, ctx_768 = _rec_inputs()

    def _L0_xattn_setup():
        import jax, jax.numpy as jnp
        import numpy as np
        B, LQ, LKV = (2, 512, 512)
        C, CTX, H, DK = (256, 192, 16, 64)
        SCALE = DK ** (-0.5)
        key = jax.random.key(seed)
        kx, ky, kq, kkv, kp, kb = jax.random.split(key, 6)
        return {'x': jax.random.normal(kx, (B, LQ, C), dtype=jnp.float32), 'y': jax.random.normal(ky, (B, LKV, CTX), dtype=jnp.float32), 'Wq': jax.random.normal(kq, (C, H * DK), dtype=jnp.float32) * C ** (-0.5), 'Wkv': jax.random.normal(kkv, (CTX, 2 * H * DK), dtype=jnp.float32) * CTX ** (-0.5), 'Wproj': jax.random.normal(kp, (H * DK, C), dtype=jnp.float32) * (H * DK) ** (-0.5), 'bproj': jax.random.normal(kb, (C,), dtype=jnp.float32) * 0.01}
    _L0_xattn_all = _L0_xattn_setup()
    _L0_xattn_in = {k: v for k, v in _L0_xattn_all.items() if k in ('Wq', 'Wkv', 'Wproj', 'bproj')}
    del _L0_xattn_all

    def _L0_ffn_setup():
        import jax, jax.numpy as jnp
        import numpy as np
        FF_DIM = 512
        TOP_K = 2
        key = jax.random.key(seed)
        k1, k2, k3, k4 = jax.random.split(key, 4)
        B, S, D, E, F = (2, 512, 256, 8, FF_DIM)
        std = 0.006
        return {'x': jax.random.normal(k1, (B, S, D), dtype=jnp.float32), 'gate_w': jax.random.normal(k2, (D, E), dtype=jnp.float32) * 0.02, 'gate_up_w': jax.random.normal(k3, (E, D, 2 * F), dtype=jnp.float32) * std, 'down_w': jax.random.normal(k4, (E, F, D), dtype=jnp.float32) * std}
    _L0_ffn_all = _L0_ffn_setup()
    _L0_ffn_in = {k: v for k, v in _L0_ffn_all.items() if k in ('gate_w', 'gate_up_w', 'down_w')}
    del _L0_ffn_all
    return {'x': x, 'ctx_768': ctx_768, 'L0_xattn_Wq': _L0_xattn_in['Wq'], 'L0_xattn_Wkv': _L0_xattn_in['Wkv'], 'L0_xattn_Wproj': _L0_xattn_in['Wproj'], 'L0_xattn_bproj': _L0_xattn_in['bproj'], 'L0_ffn_gate_w': _L0_ffn_in['gate_w'], 'L0_ffn_gate_up_w': _L0_ffn_in['gate_up_w'], 'L0_ffn_down_w': _L0_ffn_in['down_w']}

def reference(x, ctx_768, L0_xattn_Wq, L0_xattn_Wkv, L0_xattn_Wproj, L0_xattn_bproj, L0_ffn_gate_w, L0_ffn_gate_up_w, L0_ffn_down_w):
    import jax
    import jax.numpy as jnp

    def _L0_xattn_ref(x, y, Wq, Wkv, Wproj, bproj):
        import jax, jax.numpy as jnp
        import numpy as np
        B, LQ, LKV = (2, 512, 512)
        C, CTX, H, DK = (256, 192, 16, 64)
        SCALE = DK ** (-0.5)
        b, lq, _ = x.shape
        lkv = y.shape[1]
        q = (x @ Wq).reshape(b, lq, H, DK).transpose(0, 2, 1, 3)
        kv = (y @ Wkv).reshape(b, lkv, 2, H, DK).transpose(2, 0, 3, 1, 4)
        k, v = (kv[0], kv[1])
        atten = jax.nn.softmax(jnp.einsum('bhid,bhjd->bhij', q, k) * SCALE, axis=-1)
        res = jnp.einsum('bhij,bhjd->bhid', atten, v)
        res = res.transpose(0, 2, 1, 3).reshape(b, lq, H * DK)
        out = res @ Wproj + bproj
        return out

    def _L0_ffn_ref(x, gate_w, gate_up_w, down_w):
        import jax, jax.numpy as jnp
        import numpy as np
        FF_DIM = 512
        TOP_K = 2
        B, S, D = x.shape
        E = gate_up_w.shape[0]
        F = down_w.shape[1]
        x_flat = x.reshape(B * S, D)
        router_logits = x_flat @ gate_w
        router_probs = jax.nn.softmax(router_logits, axis=-1)
        top_k_probs, top_k_idx = jax.lax.top_k(router_probs, TOP_K)
        top_k_probs = top_k_probs / jnp.sum(top_k_probs, axis=-1, keepdims=True)
        gate_up = jnp.einsum('nd,edh->enh', x_flat, gate_up_w)
        gate_out = gate_up[..., :F]
        up_out = gate_up[..., F:]
        hidden = jax.nn.silu(gate_out) * up_out
        expert_out = jnp.einsum('enf,efd->end', hidden, down_w)
        out_t = jnp.transpose(expert_out, (1, 0, 2))
        sel = jnp.take_along_axis(out_t, top_k_idx[:, :, None], axis=1)
        output = jnp.sum(sel * top_k_probs[:, :, None], axis=1)
        return output.reshape(B, S, D)
    x = x + _L0_xattn_ref(_layernorm(x, axis=-1), ctx_768, L0_xattn_Wq, L0_xattn_Wkv, L0_xattn_Wproj, L0_xattn_bproj)
    x = x + _L0_ffn_ref(_layernorm(x, axis=-1), L0_ffn_gate_w, L0_ffn_gate_up_w, L0_ffn_down_w)
    return x

_drawn_inputs = setup_inputs


def setup_inputs(seed=0):
    import zlib

    import numpy as np

    out = dict(_drawn_inputs(seed))
    spreads = {}
    factors = {'L0_xattn_bproj': 6.152,
     'L0_ffn_gate_w': 8.0,
     'L0_ffn_gate_up_w': 8.0,
     'L0_ffn_down_w': 8.0}
    for name, (base, spread) in spreads.items():
        noise = np.random.default_rng([zlib.crc32(name.encode()), seed]).standard_normal(out[name].shape)
        drawn = base * np.exp(spread * noise) if base else spread * noise
        out[name] = jnp.asarray(drawn.astype(out[name].dtype))
    for name, factor in factors.items():
        out[name] = (out[name] * factor).astype(out[name].dtype)
    return out
```

```python
from contextlib import ExitStack

import numpy as np
import concourse.bass as bass
from concourse import mybir
from concourse.alu_op_type import AluOpType as ALU

F32 = mybir.dt.float32
F32R = mybir.dt.float32r
BF16 = mybir.dt.bfloat16
I32 = mybir.dt.int32
U32 = mybir.dt.uint32
ACT = mybir.ActivationFunctionType
AX = mybir.AxisListType

B, LQ, C = 32, 112, 256
LKV, CTX = 375, 192
H, DK = 16, 64
HD = H * DK
P = 128
NP = B // 2
KT, KR = 3, LKV // 3
LKE = LKV + 1
NJ = HD // P
HB = H // 2
CT = CTX - P
EPS = 1e-5
SCALE = DK ** -0.5

E, FF = 8, 512
TOK = B * LQ
CAP = TOK // P * P
assert CAP == TOK
STRIDE = CAP + P
NT = (2 * TOK + E * (P - 1)) // P
IDLE = NT - 2 * TOK // P
FJ = FF // P



def ahead(odd, step):
    out = []
    if step == 0 and odd:
        out += [("xT", 0), ("xT", 1)]
    if step % 2 == 1:
        out.append(("K", step // 2))
        if odd:
            out.append(("q", step // 2))
    if step in (2, 4, 6):
        out.append(("V", (1, step // 2 - 1)))
    if step in (10, 12, 14):
        out.append(("V", (0, step // 2 - 5)))
    if step == 8:
        out += [("yT", 0), ("yT", 1)]
    return [(odd, step, kind, a) for kind, a in out]


PAIR = [it for odd in (0, 1) for s in range(H) for it in ahead(odd, s)]
START = [(1, -1, "yT", 0), (1, -1, "yT", 1)] + [
    it for s in range(H) for it in ahead(1, s) if not (it[2] == "V" and it[3][0] == 1)]
LAST = [it for it in PAIR if it[2] not in ("q", "xT", "yT") and not (it[0] and it[2] == "K")
        and not (it[0] and it[2] == "V" and it[3][0] == 0)]


def n_split(items):
    return sum(it[2] != "V" for it in items)


class Ahead:

    def __init__(self, i):
        self.items = START if i is None else LAST if isinstance(i, int) and i == NP - 1 else PAIR
        k = 0 if i is None else i
        base = 0 if i is None else 1
        self.first = i is None
        self.n0 = base * len(START) + k * len(PAIR)
        self.split0 = base * n_split(START) + k * n_split(PAIR)
        self.v0 = base * (len(START) - n_split(START)) + k * (len(PAIR) - n_split(PAIR))
        self.bank0 = base * len(START) % 2

    def at(self, odd, step):
        return [k for k, it in enumerate(self.items) if it[0] == odd and it[1] == step]

    def find(self, odd, kind, a):
        return [k for k, it in enumerate(self.items) if (it[0], it[2], it[3]) == (odd, kind, a)][0]

    def bank(self, k):
        return (self.bank0 + k) % 2

    def made(self, k):
        return self.n0 + k + 1

    def split(self, k):
        return self.split0 + n_split(self.items[:k + 1])

    def values(self, k):
        return self.v0 + k + 1 - n_split(self.items[:k + 1])

    def split_in_pair_before(self, odd, kind, a):
        k = [n for n, it in enumerate(PAIR) if (it[0], it[2], it[3]) == (odd, kind, a)][0]
        return self.split0 - n_split(PAIR[k + 1:])

    def values_in_pair_before(self, odd, kind, a):
        k = [n for n, it in enumerate(PAIR) if (it[0], it[2], it[3]) == (odd, kind, a)][0]
        return self.v0 - (len(PAIR[k + 1:]) - n_split(PAIR[k + 1:]))


def known(v):
    return isinstance(v, int)


def there(v, end):
    return not known(v) or 0 <= v < end


def over_pairs(eng, body, first=1, end=NP - 1, tail=True):
    for i in range(first):
        body(i)
    with eng.Fori(first, end) as i:
        body(i)
    for i in range(end, NP):
        body(i)
    if tail:
        body(NP)


def over_tiles(eng, body):
    for t in range(4):
        body(t // 2, t, t % 2)
    with eng.Fori(2, NT // 2) as i:
        for k in range(2):
            body(i, 2 * i + k, k)
    body(NT // 2, NT - 1, 0)
    body(NT // 2, NT, 1)


def row_at(t, b):
    return t[:, b, :] if known(b) else t[:, bass.ds(b, 1), :].rearrange("p o k -> p (o k)")


def dram_at(t, b):
    return t[b] if known(b) else t[bass.ds(b, 1)].rearrange("o q c -> (o q) c")


def attention_and_experts(nc, x, ctx_in, Wq, Wkv, Wproj, bproj, gate_w, gate_up_w, down_w, out):
    x2_dram = nc.dram_tensor("x2_scratch", [B, LQ, C], F32).ap()
    bins = nc.dram_tensor("bins", [E * STRIDE + IDLE * P, C], F32).ap()
    y_dram = nc.dram_tensor("expert_rows", [NT * P, C], F32).ap()

    with ExitStack() as stack:
        base = (nc.sbuf_base + 63) // 64 * 64
        size = (nc.sbuf_usable_end - base) // 64 * 64 - 64
        stack.enter_context(nc.sbuf_tensor("arena", [P, size // 4], F32))
        place = {"at": base + 64}

        def sb(name, shape, dt):
            bytes_ = int(np.prod(shape[1:])) * (2 if dt == BF16 else 4)
            t = nc.alloc_sbuf_tensor_at(name, shape, dt, offset=place["at"])
            place["at"] += (bytes_ + 31) // 32 * 32
            assert place["at"] <= base + size, name
            return t

        def sem(name):
            return stack.enter_context(nc.semaphore(name))

        raw = sb("raw", [P, 2, 2048], F32)
        ident = sb("ident", [P, P], F32)
        before = sb("before", [LQ, LQ], BF16)
        ones = sb("ones", [LQ, P], BF16)
        iota_e = sb("iota_e", [P, E], F32)
        le_mask = sb("le_mask", [P, E, E], F32)
        iota_tile = sb("iota_tile", [P, CAP // P], F32)
        iota_t = sb("iota_t", [P, NT], F32)
        iota_p = sb("iota_p", [P, E], F32)
        zero = sb("zero", [P, C], F32)
        running = sb("running", [P, E], F32)
        choice = sb("choice", [LQ, B, 2], F32)
        rank = sb("rank", [LQ, B, 2], F32)
        share = sb("share", [LQ, B, 2], F32)
        row_of = sb("row_of", [LQ, B, 2], I32)
        tile_row = sb("tile_row", [P, NT], I32)
        tile_expert = sb("tile_expert", [P, NT], I32)
        row_now = sb("row_now", [LQ, 2, 2], I32)
        pad_row = sb("pad_row", [P, E], I32)
        shared_from = place["at"]

        WqH = sb("WqH", [P, 2, HD], F32R)
        WqL = sb("WqL", [P, 2, HD], F32R)
        WkvH = sb("WkvH", [P, 2 * HD], F32R)
        WkvL = sb("WkvL", [P, 2 * HD], F32R)
        WkvT = sb("WkvT", [P, 2 * HD], F32R)
        WkvU = sb("WkvU", [CT, 2 * HD], F32R)
        WpH = sb("WpH", [P, NJ, C], F32R)
        WpL = sb("WpL", [P, NJ, C], F32R)
        gw = sb("gw", [P, 2, E], F32)
        bias = sb("bias", [LQ, C], F32)
        y_sb = sb("y_sb", [KR, 2, KT, 2 * P], F32)
        yA_h = sb("yA_h", [P, 2, LKE], F32R)
        yA_l = sb("yA_l", [P, 2, LKE], F32R)
        yB = sb("yB", [P, 2, LKE], F32R)
        K_h = sb("K_h", [P, NJ, LKE], F32R)
        K_l = sb("K_l", [P, NJ, LKE], F32R)
        q_h = sb("q_h", [P, NJ, 2 * LQ], F32R)
        q_l = sb("q_l", [P, NJ, 2 * LQ], F32R)
        V = sb("V", [KR, KT, HD], F32)
        prob = sb("prob", [LQ, 2, LKV], F32)
        probT = sb("probT", [KR, 2, KT * LQ], F32)
        neg_max = sb("neg_max", [LQ, 2], F32)
        row_sum = sb("row_sum", [LQ, 2, HB], F32)
        inv_sum = sb("inv_sum", [LQ, HB], F32)
        O_sb = sb("O_sb", [LQ, HD], F32)
        OT_h = sb("OT_h", [P, NJ, LQ], F32R)
        OT_l = sb("OT_l", [P, NJ, LQ], F32R)
        x_sb = sb("x_sb", [LQ, 2, C], F32)
        xn = sb("xn", [LQ, 2, C], F32)
        xT_h = sb("xT_h", [P, 2, 2 * LQ], F32R)
        xT_l = sb("xT_l", [P, 2, 2 * LQ], F32R)
        stat1 = sb("stat1", [LQ, 2, 6], F32)
        mv1 = sb("mv1", [LQ, 2, 2], F32)
        std1 = sb("std1", [LQ, 2, 2], F32)
        x_res = sb("x_res", [LQ, 2, C], F32)
        x_bias = sb("x_bias", [LQ, 2, C], F32)
        x2 = sb("x2", [LQ, 2, C], F32)
        hn = sb("hn", [LQ, 2, C], F32)
        stat2 = sb("stat2", [LQ, 6], F32)
        mv2 = sb("mv2", [LQ, 2], F32)
        std2 = sb("std2", [LQ, 2], F32)
        minus_half = sb("minus_half", [LQ, 2], F32)
        hnT = sb("hnT", [P, 2, LQ], F32)
        neg_top = sb("neg_top", [LQ, 1], F32)
        gates = sb("gates", [LQ, E], F32)
        top = sb("top", [LQ, E], F32)
        top_i = sb("top_i", [LQ, E], U32)
        top_f = sb("top_f", [LQ, 2], F32)
        onehot = sb("onehot", [LQ, 2, E], F32)
        chosen = sb("chosen", [LQ, E], BF16)
        bin_at = sb("bin_at", [LQ, E], F32)
        picked = sb("picked", [LQ, 2, E], F32)
        rank2 = sb("rank2", [LQ, 2], F32)
        bin_row = sb("bin_row", [LQ, 2, 2], I32)
        top_sum = sb("top_sum", [LQ, 1], F32)
        inv_top = sb("inv_top", [LQ, 1], F32)

        place["at"] = shared_from
        Wd = sb("Wd", [P, E, FJ, C], F32)
        Wgu = sb("Wgu", [P, E, 2, 2, 2 * FF], F32R)
        h_in = sb("h_in", [P, 2, C], F32)
        hT_h = sb("hT_h", [P, 2, P], F32R)
        hT_l = sb("hT_l", [P, 2, P], F32R)
        silu = sb("silu", [P, FF], F32)
        hid = sb("hid", [P, FF], F32)
        hidT = sb("hidT", [P, FJ, P], F32)
        y_out = sb("y_out", [P, 2, C], F32)
        place["at"] = shared_from
        t_cmp = sb("t_cmp", [P, E, CAP // P], F32)
        n_tiles = sb("n_tiles", [P, E], F32)
        t_ee = sb("t_ee", [P, E, E], F32)
        cum = sb("cum", [P, E], F32)
        cum_ex = sb("cum_ex", [P, E], F32)
        t_te = sb("t_te", [P, NT, E], F32)
        t_tc = sb("t_tc", [P, NT, E], F32)
        e_of = sb("e_of", [P, NT], F32)
        prev = sb("prev", [P, NT], F32)
        within = sb("within", [P, NT], F32)
        t_be = sb("t_be", [LQ, 2 * B, E], F32)
        t_bc = sb("t_bc", [LQ, 2 * B, E], F32)
        first_tile = sb("first_tile", [LQ, 2 * B], F32)
        place["at"] = shared_from
        g_rows = sb("g_rows", [LQ, 2, 2, C], F32)
        g_x = sb("g_x", [LQ, 2, C], F32)
        g_sum = sb("g_sum", [LQ, 2, C], F32)
        g_out = sb("g_out", [LQ, 2, C], F32)

        banks = [stack.enter_context(nc.psum_tensor(f"bank{k}", [P, 512], F32)) for k in range(8)]
        S_ps, PT_ps, A_ps, O_ps, C_ps = banks[0:2], banks[2:4], banks[4:6], banks[6], banks[7]
        gate_ps, up_ps, hT_ps, hidT_ps = banks[0:2], banks[2:4], banks[4], banks[5]
        down_ps = banks[6:8]

        raw_in = [sem(f"raw_in{k}") for k in range(2)]
        small_in = sem("small_in")
        consts = sem("consts")
        passed = sem("passed")
        w_hi, w_lo = sem("w_hi"), sem("w_lo")
        y_in = [sem(f"y_in{k}") for k in range(2)]
        x_in = sem("x_in")
        xres_in = [sem(f"xres_in{k}") for k in range(2)]
        made = sem("made")
        hi_done, lo_done = sem("hi_done"), sem("lo_done")
        v_done = sem("v_done")
        scores_made, max_done, exp_done = sem("scores_made"), sem("max_done"), sem("exp_done")
        probT_made = sem("probT_made")
        probT_even, probT_odd = sem("probT_even"), sem("probT_odd")
        pv_made = sem("pv_made")
        inv_done, O_done = sem("inv_done"), sem("O_done")
        OT_made, OT_hi, OT_lo = sem("OT_made"), sem("OT_hi"), sem("OT_lo")
        proj_made, x2_done, x2_out = sem("proj_made"), sem("x2_done"), [sem("x2_out0"), sem("x2_out1")]
        st1, ag1, eps1, rs1, xn_done = sem("st1"), sem("ag1"), sem("eps1"), sem("rs1"), sem("xn_done")
        xb_done = sem("xb_done")
        st2, ag2, eps2, rs2, hn_done = sem("st2"), sem("ag2"), sem("eps2"), sem("rs2"), sem("hn_done")
        hnT_made, hnT_done = sem("hnT_made"), sem("hnT_done")
        logits_made, top_neg, gates_done = sem("logits_made"), sem("top_neg"), sem("gates_done")
        top_done, topi_done, topf_done = sem("top_done"), sem("topi_done"), sem("topf_done")
        onehot_done, chosen_done = sem("onehot_done"), sem("chosen_done")
        counts_made, binat_done, running_done = sem("counts_made"), sem("binat_done"), sem("running_done")
        picked_done, rank_done, row_done = sem("picked_done"), sem("rank_done"), sem("row_done")
        tsum_done, tinv_done = sem("tsum_done"), sem("tinv_done")
        kept = sem("kept")
        scattered = [sem("scattered0"), sem("scattered1")]
        idle_out, pads_out = sem("idle_out"), sem("pads_out")
        plan = sem("plan")
        wd_in = sem("wd_in")
        wgu_raw = [sem("wgu_raw0"), sem("wgu_raw1")]
        wgu_hi, wgu_lo = sem("wgu_hi"), sem("wgu_lo")
        h_in_ld = [sem("h_in0"), sem("h_in1")]
        hT_made, hT_hi, hT_lo = sem("hT_made"), sem("hT_hi"), sem("hT_lo")
        gate_made, up_made, silu_done, hid_done = sem("gate_made"), sem("up_made"), sem("silu_done"), sem("hid_done")
        hidT_made, hidT_done, down_made, y_done = sem("hidT_made"), sem("hidT_done"), sem("down_made"), sem("y_done")
        y_store = [sem("y_store0"), sem("y_store1")]
        g_in = [sem("g_in0"), sem("g_in1")]
        gx_in = [sem("gx_in0"), sem("gx_in1")]
        row_ready = sem("row_ready")
        gsum_done, gout_done = sem("gsum_done"), sem("gout_done")
        out_store = [sem("out_store0"), sem("out_store1")]

        N_CONSTS = 17
        N_PLAN = 18
        block = stack.enter_context(nc.Block())

        @block.sync
        def _(sp):
            def load_y(b, slot):
                rows = ctx_in[b:b + 1] if known(b) else ctx_in[bass.ds(b, 1)]
                rows = rows.rearrange("o (k p) c -> p (o k) c", p=KR)
                sp.dma_start(y_sb[:, slot, :, 0:CTX], rows).then_inc(y_in[slot], 16)
                sp.dma_start(y_sb[:, slot, :, CTX:2 * P], rows[:, :, P:CTX]).then_inc(y_in[slot], 16)

            def load_x(pair):
                rows = x[bass.ds(2 * pair, 2)] if not known(pair) else x[2 * pair:2 * pair + 2]
                sp.dma_start(x_sb[:], rows.rearrange("b q c -> q b c")).then_inc(x_in, 16)

            sp.sem_inc(x2_out[1], 16)
            load_y(0, 0)
            sp.dma_start(raw[:, 0, :], Wkv[0:P, :]).then_inc(raw_in[0], 16)
            load_x(0)
            sp.dma_start(raw[0:CT, 1, :], Wkv[P:CTX, :]).then_inc(raw_in[1], 16)
            sp.dma_start(raw[CT:P, 1, :], Wkv[P:CTX, :]).then_inc(raw_in[1], 16)
            load_y(1, 1)
            sp.dma_start(gw[:], gate_w.rearrange("(k p) e -> p k e", p=P)).then_inc(small_in, 16)
            sp.dma_start(bias[:], bproj.rearrange("(o c) -> o c", o=1).to_broadcast([LQ, C])).then_inc(small_in, 16)
            sp.wait_ge(w_lo, 1)
            sp.dma_start(raw[:, 0, :], Wq.rearrange("(k p) n -> p k n", p=P)).then_inc(raw_in[0], 16)
            sp.wait_ge(w_lo, 2)
            sp.dma_start(raw[:, 1, :], Wproj.rearrange("(k p) n -> p k n", p=P)).then_inc(raw_in[1], 16)
            a = Ahead(None)
            sp.wait_ge(made, a.made(1))
            load_y(2, 0)
            sp.wait_ge(xn_done, 2)
            load_x(1)
            sp.wait_ge(made, a.made([k for k, it in enumerate(START) if it[2:] == ("yT", 1)][1]))
            load_y(3, 1)
            sp.wait_ge(consts, 1)
            for k in range(IDLE):
                r = E * STRIDE + k * P
                sp.dma_start(bins[r:r + P, :], zero[:]).then_inc(idle_out, 16)

            def pair(i):
                a = Ahead(i)
                for odd in (0, 1):
                    b = 2 * i + odd
                    if there(b, B):
                        if not known(b) or b >= 2:
                            sp.wait_ge(xb_done, b - 1)
                        sp.dma_start(x_res[:, odd, :], dram_at(x, b)).then_inc(xres_in[odd], 16)
                    if there(b - 1, B):
                        sp.wait_ge(x2_done, b)
                        sp.dma_start(dram_at(x2_dram, b - 1), x2[:, 1 - odd, :]).then_inc(x2_out[1 - odd], 16)
                    if not known(i) or i + 2 < NP:
                        sp.wait_ge(made, a.made(a.find(odd, "yT", 1)))
                        load_y(b + 4, odd)
                    if odd and (not known(i) or i + 2 < NP):
                        sp.wait_ge(xn_done, 2 * (i + 2))
                        load_x(i + 2)

            over_pairs(sp, pair, 1, NP - 2)

            sp.wait_ge(plan, N_PLAN)
            sp.wait_ge(counts_made, B)
            sp.wait_ge(gates_done, B)
            sp.wait_ge(x2_out[0], 16 * NP)
            sp.wait_ge(x2_out[1], 16 * NP + 16)
            sp.wait_ge(scattered[0], 32 * NP)
            sp.wait_ge(scattered[1], 32 * NP)
            for e in range(E):
                if e >= 2:
                    sp.wait_ge(wgu_lo, e - 1)
                sp.dma_start(raw[:, e % 2, :].rearrange("p (k n) -> p k n", k=2),
                             gate_up_w[e].rearrange("(k p) n -> p k n", p=P)).then_inc(wgu_raw[e % 2], 16)
                sp.dma_start(Wd[:, e], down_w[e].rearrange("(k p) n -> p k n", p=P)).then_inc(wd_in, 16)
                if e == 0:
                    sp.wait_ge(pads_out, 16 * E)
                    sp.wait_ge(idle_out, 16 * IDLE)

            def load_rows(t, slot):
                r = sp.value_load(tile_row[0:1, t:t + 1] if known(t) else tile_row[0:1, bass.ds(t, 1)],
                                  min_val=0, max_val=E * STRIDE + (IDLE - 1) * P)
                sp.dma_start(h_in[:, slot, :], bins[bass.ds(r, P), :]).then_inc(h_in_ld[slot], 16)

            load_rows(0, 0)

            def tile(i, t, k):
                if there(t + 1, NT):
                    if not known(t) or t >= 1:
                        sp.wait_ge(hT_made, t)
                    load_rows(t + 1, 1 - k)
                if there(t - 1, NT):
                    sp.wait_ge(y_done, t)
                    rows = y_dram[(t - 1) * P:t * P, :] if known(t) else y_dram[bass.ds(t * P - P, P), :]
                    sp.dma_start(rows, y_out[:, 1 - k, :]).then_inc(y_store[1 - k], 16)

            over_tiles(sp, tile)

            for k in range(2):
                sp.wait_ge(y_store[k], 16 * ((NT + 1 - k) // 2))

            def last_pair(i):
                for k in range(2):
                    b = 2 * i + k
                    if not known(i) or i > 0:
                        sp.wait_ge(gsum_done, b - 1)
                    sp.dma_start(g_x[:, k, :], dram_at(x2_dram, b)).then_inc(gx_in[k], 16)
                for k in range(2):
                    b = 2 * i + k
                    sp.wait_ge(gout_done, b + 1)
                    sp.dma_start(dram_at(out, b), g_out[:, k, :]).then_inc(out_store[k], 16)

            last_pair(0)
            with sp.Fori(1, NP) as i:
                last_pair(i)
            for k in range(2):
                sp.wait_ge(out_store[k], 16 * NP)

        @block.gpsimd
        def _(pool):
            pool.memset(zero[:], 0.0).then_inc(consts, 1)
            pool.memset(ident[:], 0.0).then_inc(consts, 1)
            pool.memset(before[:], 1.0).then_inc(consts, 1)
            pool.memset(ones[:], 1.0).then_inc(consts, 1)
            pool.memset(le_mask[:], 1.0).then_inc(consts, 1)
            pool.memset(minus_half[:], -0.5).then_inc(consts, 1)
            pool.memset(running[:], 0.0).then_inc(consts, 1)
            for t in (yA_h, yA_l, yB):
                pool.memset(t[:, :, LKV:LKE].bitcast(F32), 0.0).then_inc(consts, 1)
            pool.iota(iota_e[:], [[1, E]], base=0, channel_multiplier=0,
                      allow_small_or_imprecise_dtypes=True).then_inc(consts, 1)
            pool.iota(iota_tile[:], [[P, CAP // P]], base=0, channel_multiplier=0,
                      allow_small_or_imprecise_dtypes=True).then_inc(consts, 1)
            pool.iota(iota_t[:], [[1, NT]], base=0, channel_multiplier=0,
                      allow_small_or_imprecise_dtypes=True).then_inc(consts, 1)
            pool.iota(iota_p[:], [[STRIDE, E]], base=0, channel_multiplier=1,
                      allow_small_or_imprecise_dtypes=True).then_inc(consts, 1)
            pool.wait_ge(consts, N_CONSTS - 3)
            pool.affine_select(out=ident[:], in_=ident[:], compare_op=ALU.not_equal, fill=1.0, base=0,
                               pattern=[[-1, P]], channel_multiplier=1).then_inc(consts, 1)
            pool.affine_select(out=before[:], in_=before[:], compare_op=ALU.is_gt, fill=0.0, base=0,
                               pattern=[[1, LQ]], channel_multiplier=-1).then_inc(consts, 1)
            pool.affine_select(out=le_mask[:], in_=le_mask[:], compare_op=ALU.is_ge, fill=0.0, base=0,
                               pattern=[[1, E], [-1, E]], channel_multiplier=0).then_inc(consts, 1)

            def norm_x(pair):
                pool.wait_ge(ag1, 2 * pair + 2)
                pool.sem_inc(passed, 1)
                pool.tensor_scalar(std1[:, :, 0], mv1[:, :, 1], EPS, None, ALU.add).then_inc(eps1, 1)
                pool.wait_ge(eps1, pair + 1)
                pool.tensor_tensor(std1[:, :, 1], std1[:, :, 0], minus_half[:, 0:2], ALU.pow).then_inc(rs1, 1)
                if not known(pair) or pair > 0:
                    a = Ahead(pair - 2 if not known(pair) or pair > 1 else None)
                    pool.wait_ge(made, a.made(a.find(1, "xT", 1)))
                pool.wait_ge(rs1, pair + 1)
                pool.sem_inc(passed, 1)
                for r in range(2):
                    pool.tensor_scalar(xn[:, r, :], x_sb[:, r, :], mv1[:, r, 0:1], std1[:, r, 1:2],
                                       ALU.subtract, ALU.mult).then_inc(xn_done, 1)

            norm_x(0)

            def scatter(b, slot):
                pool.wait_ge(row_done, b + 1)
                pool.sem_inc(passed, 1)
                for k in range(2):
                    pool.indirect_dma_start(bins, bass.IndirectOffsetOnAxis(ap=bin_row[:, slot, k:k + 1], axis=0),
                                            hn[:, slot, :], None).then_inc(scattered[slot], 16)

            def pair(i):
                for odd in (0, 1):
                    b = 2 * i + odd
                    if there(b, B):
                        pool.wait_ge(xres_in[odd], 16 * (i + 1))
                        if known(b) and b == 0:
                            pool.wait_ge(small_in, 32)
                        if not known(b) or b >= 2:
                            pool.wait_ge(x2_done, b - 1)
                        pool.tensor_tensor(x_bias[:, odd, :], x_res[:, odd, :], bias[:], ALU.add).then_inc(xb_done, 1)
                    if there(b - 2, B):
                        scatter(b - 2, odd)
                    if there(b - 1, B):
                        pool.wait_ge(ag2, b)
                        pool.sem_inc(passed, 1)
                        pool.tensor_scalar(std2[:, 0:1], mv2[:, 1:2], EPS, None, ALU.add).then_inc(eps2, 1)
                        pool.wait_ge(eps2, b)
                        pool.tensor_tensor(std2[:, 1:2], std2[:, 0:1], minus_half[:, 0:1], ALU.pow).then_inc(rs2, 1)
                        if not known(b) or b >= 3:
                            pool.wait_ge(scattered[1 - odd], 32 * (i - 1 + odd))
                        pool.wait_ge(rs2, b)
                        pool.sem_inc(passed, 1)
                        pool.tensor_scalar(hn[:, 1 - odd, :], x2[:, 1 - odd, :], mv2[:, 0:1], std2[:, 1:2],
                                           ALU.subtract, ALU.mult).then_inc(hn_done, 1)
                    if not odd and (not known(i) or i + 1 < NP):
                        norm_x(i + 1)

            over_pairs(pool, pair, 2)

            pool.wait_ge(plan, 1)
            for e in range(E):
                pool.indirect_dma_start(bins, bass.IndirectOffsetOnAxis(ap=pad_row[:, e:e + 1], axis=0),
                                        zero[:], None).then_inc(pads_out, 16)

            pool.wait_ge(plan, N_PLAN)
            pool.wait_ge(counts_made, B)
            pool.wait_ge(gates_done, B)
            for k in range(2):
                pool.wait_ge(scattered[k], 32 * NP)
            for e in range(E):
                pool.wait_ge(wgu_raw[e % 2], 16 * (e // 2 + 1))
                src = raw[:, e % 2, :].rearrange("p (k n) -> p k n", k=2)
                pool.tensor_copy(Wgu[:, e, 0], src).then_inc(wgu_hi, 1)
                pool.wait_ge(wgu_hi, e + 1)
                pool.tensor_tensor(Wgu[:, e, 1], src, Wgu[:, e, 0].bitcast(F32), ALU.subtract).then_inc(wgu_lo, 1)

            for k in range(2):
                pool.wait_ge(y_store[k], 16 * ((NT + 1 - k) // 2))

            def last_pair(i):
                for s in range(2):
                    b = 2 * i + s
                    if not known(i) or i > 0:
                        pool.wait_ge(g_in[s], 32 * i)
                        pool.wait_ge(gout_done, b - 1)
                    pool.tensor_copy(row_now[:, s, :], row_at(row_of, b)).then_inc(row_ready, 1)
                    pool.wait_ge(row_ready, b + 1)
                    pool.sem_inc(passed, 1)
                    for k in range(2):
                        pool.indirect_dma_start(g_rows[:, s, k, :], None, y_dram,
                                                bass.IndirectOffsetOnAxis(ap=row_now[:, s, k:k + 1], axis=0)).then_inc(g_in[s], 16)

            last_pair(0)
            with pool.Fori(1, NP) as i:
                last_pair(i)

        @block.scalar
        def _(act):
            def hi_of_weight(dst, slot, loads, scale=1.0):
                act.wait_ge(raw_in[slot], 16 * loads)
                nc.scalar.mul(dst, raw[:, slot, :], scale).then_inc(w_hi, 1)

            def evacuate(a, k):
                odd, step, kind, arg = a.items[k]
                src = A_ps[a.bank(k)]
                act.wait_ge(made, a.made(k))
                if kind == "V":
                    half, t = arg
                    nc.scalar.copy(V[:, t, half * 512:half * 512 + 512], src[0:KR, :]).then_inc(v_done, 1)
                elif kind == "K":
                    nc.scalar.copy(K_h[:, arg, :], src[:, 0:LKE]).then_inc(hi_done, 1)
                elif kind == "q":
                    nc.scalar.copy(q_h[:, arg, :], src[:, 0:2 * LQ]).then_inc(hi_done, 1)
                elif kind == "yT":
                    slot = 0 if step < 0 else odd
                    dst = (yA_h if arg == 0 else yB)[:, slot, 0:LKV]
                    nc.scalar.copy(dst, src[:, 0:LKV]).then_inc(hi_done, 1)
                else:
                    nc.scalar.copy(xT_h[:, :, arg * LQ:arg * LQ + LQ],
                                   src[:, 0:2 * LQ].rearrange("p (k q) -> p k q", k=2)).then_inc(hi_done, 1)

            a = Ahead(None)
            evacuate(a, 0)
            evacuate(a, 1)
            hi_of_weight(WkvH[:], 0, 1)
            hi_of_weight(WkvT[:], 1, 2)
            evacuate(a, 2)
            evacuate(a, 3)
            hi_of_weight(WqH[:].rearrange("p k n -> p (k n)"), 0, 2, SCALE)
            for k in range(4, len(a.items)):
                evacuate(a, k)
            hi_of_weight(WpH[:].rearrange("p k n -> p (k n)"), 1, 3)

            def pair(i):
                a = Ahead(i) if there(i, NP) else None
                for odd in (0, 1):
                    b = 2 * i + odd
                    for s in range(H):
                        g = H * b + s
                        if there(g, B * H):
                            act.wait_ge(max_done, g + 1)
                            if not known(g) or g >= 2:
                                act.wait_ge(probT_made, g - 1)
                            nc.scalar.activation(prob[:, s % 2, :], S_ps[s % 2][0:LQ, 0:LKV], ACT.Exp,
                                                 bias=neg_max[:, s % 2:s % 2 + 1],
                                                 accum_out=row_sum[:, s // HB, s % HB:s % HB + 1]).then_inc(exp_done, 1)
                        for k in (a.at(odd, s) if a else ()):
                            evacuate(a, k)
                        if s % 2 == 1 and there(g - 1, B * H):
                            act.wait_ge(probT_made, g)
                            if not known(g) or g >= 3:
                                act.wait_ge(pv_made, g - 2)
                            nc.scalar.copy(probT[:, 0, :], PT_ps[0][0:KR, 0:KT * LQ]).then_inc(probT_even, 1)
                        if s in (3, 11) and there(b - (s == 3), B):
                            half = s == 3
                            n = 2 * (b - half) + half
                            act.wait_ge(OT_made, n + 1)
                            nc.scalar.copy(OT_h[:, 4 * half:4 * half + 4, :].rearrange("p j q -> p (j q)"),
                                           C_ps[:, 0:4 * LQ]).then_inc(OT_hi, 1)
                        if s == 13 and there(b - 1, B):
                            act.wait_ge(top_neg, b)
                            nc.scalar.activation(gates[:], C_ps[0:LQ, 0:E], ACT.Exp,
                                                 bias=neg_top[:, 0:1]).then_inc(gates_done, 1)

            over_pairs(act, pair)

            act.wait_ge(plan, N_PLAN)

            def hi_of_rows(t):
                act.wait_ge(hT_made, t + 1)
                nc.scalar.copy(hT_h[:].rearrange("p k n -> p (k n)"), hT_ps[:, 0:2 * P]).then_inc(hT_hi, 1)

            hi_of_rows(0)

            def tile(i, t, k):
                if there(t, NT):
                    act.wait_ge(gate_made, t + 1)
                    if not known(t) or t >= 1:
                        act.wait_ge(hid_done, t)
                    nc.scalar.activation(silu[:], gate_ps[k][:], ACT.Silu).then_inc(silu_done, 1)
                if there(t + 1, NT):
                    hi_of_rows(t + 1)
                if there(t - 1, NT):
                    act.wait_ge(down_made, t)
                    if not known(t) or t >= 3:
                        act.wait_ge(y_store[1 - k], 16 * (i - 1 + k))
                    nc.scalar.copy(y_out[:, 1 - k, :], down_ps[1 - k][:, 0:C]).then_inc(y_done, 1)

            over_tiles(act, tile)

        @block.vector
        def _(dve):
            def norm_x(pair):
                dve.wait_ge(x_in, 16 * (pair + 1))
                if not known(pair) or pair > 0:
                    dve.wait_ge(xn_done, 2 * pair)
                for r in range(2):
                    nc.vector.bn_stats(stat1[:, r, :], x_sb[:, r, :]).then_inc(st1, 1)
                for r in range(2):
                    dve.wait_ge(st1, 2 * pair + 1 + r)
                    dve.sem_inc(passed, 1)
                    nc.vector.bn_aggr(mv1[:, r, :], stat1[:, r, :]).then_inc(ag1, 1)

            def low_part(a, k):
                odd, step, kind, arg = a.items[k]
                if kind == "V":
                    return
                src = A_ps[a.bank(k)]
                dve.wait_ge(hi_done, a.split(k))
                if kind == "K":
                    lo, ps, hi = K_l[:, arg, :], src[:, 0:LKE], K_h[:, arg, :]
                elif kind == "q":
                    lo, ps, hi = q_l[:, arg, :], src[:, 0:2 * LQ], q_h[:, arg, :]
                elif kind == "yT":
                    slot = 0 if step < 0 else odd
                    if arg == 0:
                        lo, ps, hi = yA_l[:, slot, 0:LKV], src[:, 0:LKV], yA_h[:, slot, 0:LKV]
                    else:
                        lo, ps, hi = yB[CT:P, slot, 0:LKV], src[CT:P, 0:LKV], yB[CT:P, slot, 0:LKV]
                else:
                    lo, hi = xT_l[:, :, arg * LQ:arg * LQ + LQ], xT_h[:, :, arg * LQ:arg * LQ + LQ]
                    ps = src[:, 0:2 * LQ].rearrange("p (k q) -> p k q", k=2)
                nc.vector.tensor_tensor(lo, ps, hi.bitcast(F32), ALU.subtract).then_inc(lo_done, 1)

            a = Ahead(None)
            low_part(a, 0)
            low_part(a, 1)
            norm_x(0)
            dve.wait_ge(w_hi, 1)
            nc.vector.tensor_tensor(WkvL[:], raw[:, 0, :], WkvH[:].bitcast(F32), ALU.subtract).then_inc(w_lo, 1)
            dve.wait_ge(w_hi, 2)
            nc.vector.tensor_tensor(WkvU[:], raw[0:CT, 1, :], WkvT[0:CT, :].bitcast(F32), ALU.subtract).then_inc(w_lo, 1)
            low_part(a, 2)
            low_part(a, 3)
            dve.wait_ge(w_hi, 3)
            nc.vector.scalar_tensor_tensor(WqL[:].rearrange("p k n -> p (k n)"), raw[:, 0, :], SCALE,
                                           WqH[:].rearrange("p k n -> p (k n)").bitcast(F32),
                                           ALU.mult, ALU.subtract).then_inc(w_lo, 1)
            for k in range(4, len(a.items)):
                low_part(a, k)
            dve.wait_ge(w_hi, 4)
            nc.vector.tensor_tensor(WpL[:].rearrange("p k n -> p (k n)"), raw[:, 1, :],
                                    WpH[:].rearrange("p k n -> p (k n)").bitcast(F32), ALU.subtract).then_inc(w_lo, 1)

            def normalise(n, k):
                dve.wait_ge(exp_done, HB * n + HB)
                nc.vector.reciprocal(inv_sum[:], row_sum[:, k, :]).then_inc(inv_done, 1)
                dve.wait_ge(inv_done, n + 1)
                dve.wait_ge(pv_made, HB * n + HB)
                nc.vector.tensor_tensor(O_sb[:, k * 512:k * 512 + 512].rearrange("p (h d) -> p h d", h=HB),
                                        O_ps[0:LQ, :].rearrange("p (h d) -> p h d", h=HB),
                                        inv_sum[:].unsqueeze(2).to_broadcast([LQ, HB, DK]),
                                        ALU.mult).then_inc(O_done, 1)

            def residual(i, b, slot):
                dve.wait_ge(proj_made, b + 1)
                dve.wait_ge(xb_done, b + 1)
                if not known(b) or b >= 2:
                    dve.wait_ge(x2_out[slot], 16 * i)
                nc.vector.tensor_tensor(x2[:, slot, :], C_ps[0:LQ, 0:C], x_bias[:, slot, :], ALU.add).then_inc(x2_done, 1)
                dve.wait_ge(x2_done, b + 1)
                nc.vector.bn_stats(stat2[:], x2[:, slot, :]).then_inc(st2, 1)
                dve.wait_ge(st2, b + 1)
                dve.sem_inc(passed, 1)
                nc.vector.bn_aggr(mv2[:], stat2[:]).then_inc(ag2, 1)

            def choose(b):
                dve.wait_ge(gates_done, b + 1)
                dve.sem_inc(passed, 1)
                nc.vector.max(top[:], gates[:]).then_inc(top_done, 1)
                dve.wait_ge(top_done, b + 1)
                dve.sem_inc(passed, 1)
                nc.vector.max_index(top_i[:], top[:], gates[:]).then_inc(topi_done, 1)

            def mark(b):
                dve.wait_ge(topi_done, b + 1)
                nc.vector.tensor_copy(top_f[:], top_i[:, 0:2]).then_inc(topf_done, 1)
                nc.vector.tensor_reduce(top_sum[:], top[:, 0:2], AX.X, ALU.add).then_inc(tsum_done, 1)
                dve.wait_ge(topf_done, b + 1)
                nc.vector.tensor_tensor(onehot[:], iota_e[0:LQ, :].unsqueeze(1).to_broadcast([LQ, 2, E]),
                                        top_f[:].unsqueeze(2).to_broadcast([LQ, 2, E]),
                                        ALU.is_equal).then_inc(onehot_done, 1)
                dve.wait_ge(tsum_done, b + 1)
                nc.vector.reciprocal(inv_top[:], top_sum[:]).then_inc(tinv_done, 1)
                dve.wait_ge(onehot_done, b + 1)
                nc.vector.tensor_tensor(chosen[:], onehot[:, 0, :], onehot[:, 1, :], ALU.add).then_inc(chosen_done, 1)
                dve.wait_ge(tinv_done, b + 1)
                nc.vector.tensor_scalar(row_at(share, b), top[:, 0:2], inv_top[:, 0:1], None, ALU.mult).then_inc(kept, 1)

            def assign(b, slot):
                dve.wait_ge(counts_made, b + 1)
                nc.vector.tensor_tensor(bin_at[:], C_ps[0:LQ, 0:E], running[0:LQ, :], ALU.add).then_inc(binat_done, 1)
                dve.wait_ge(binat_done, b + 1)
                nc.vector.tensor_tensor(running[:], C_ps[:, E:2 * E], running[:], ALU.add).then_inc(running_done, 1)
                nc.vector.tensor_tensor(picked[:], onehot[:], bin_at[:].unsqueeze(1).to_broadcast([LQ, 2, E]),
                                        ALU.mult).then_inc(picked_done, 1)
                dve.wait_ge(picked_done, b + 1)
                nc.vector.tensor_reduce(rank2[:], picked[:], AX.X, ALU.add).then_inc(rank_done, 1)
                dve.wait_ge(rank_done, b + 1)
                nc.vector.scalar_tensor_tensor(bin_row[:, slot, :], top_f[:], float(STRIDE), rank2[:],
                                               ALU.mult, ALU.add).then_inc(row_done, 1)
                nc.vector.tensor_copy(row_at(rank, b), rank2[:]).then_inc(kept, 1)
                nc.vector.tensor_copy(row_at(choice, b), top_f[:]).then_inc(kept, 1)

            def pair(i):
                a = Ahead(i) if there(i, NP) else None
                for odd in (0, 1):
                    b = 2 * i + odd
                    for s in range(H):
                        g = H * b + s
                        if there(g, B * H):
                            dve.wait_ge(scores_made, g + 1)
                            nc.vector.tensor_reduce(neg_max[:, s % 2:s % 2 + 1], S_ps[s % 2][0:LQ, 0:LKV],
                                                    AX.X, ALU.max, negate=True).then_inc(max_done, 1)
                        if s == 2 and there(b - 1, B):
                            normalise(2 * b - 1, 1)
                        if s == 10 and there(b, B):
                            normalise(2 * b, 0)
                        for k in (a.at(odd, s) if a else ()):
                            low_part(a, k)
                        if s % 2 == 0 and there(g - 1, B * H):
                            dve.wait_ge(probT_made, g)
                            if not known(g) or g >= 3:
                                dve.wait_ge(pv_made, g - 2)
                            nc.vector.tensor_copy(probT[:, 1, :], PT_ps[1][0:KR, 0:KT * LQ]).then_inc(probT_odd, 1)
                        if s in (3, 11) and there(b - (s == 3), B):
                            half = int(s == 3)
                            dve.wait_ge(OT_hi, 2 * (b - half) + half + 1)
                            nc.vector.tensor_tensor(OT_l[:, 4 * half:4 * half + 4, :].rearrange("p j q -> p (j q)"),
                                                    C_ps[:, 0:4 * LQ],
                                                    OT_h[:, 4 * half:4 * half + 4, :].rearrange("p j q -> p (j q)").bitcast(F32),
                                                    ALU.subtract).then_inc(OT_lo, 1)
                        if s == 1 and there(b - 2, B):
                            assign(b - 2, odd)
                        if s == 5 and there(b - 1, B):
                            residual(i, b - 1, 1 - odd)
                        if s == 8 and there(b - 1, B):
                            dve.wait_ge(hnT_made, b)
                            nc.vector.tensor_copy(hnT[:].rearrange("p k q -> p (k q)"), C_ps[:, 0:2 * LQ]).then_inc(hnT_done, 1)
                        if s == 12 and not odd and (not known(i) or i + 1 < NP):
                            norm_x(i + 1)
                        if there(b - 1, B):
                            if s == 13:
                                dve.wait_ge(logits_made, b)
                                nc.vector.tensor_reduce(neg_top[:], C_ps[0:LQ, 0:E], AX.X, ALU.max,
                                                        negate=True).then_inc(top_neg, 1)
                            if s == 14:
                                choose(b - 1)
                            if s == 15:
                                mark(b - 1)

            over_pairs(dve, pair)

            done = [0]

            def step(ins):
                done[0] += 1
                ins.then_inc(plan, 1)
                dve.wait_ge(plan, done[0])

            dve.wait_ge(running_done, B)
            dve.wait_ge(kept, 3 * B)
            step(nc.vector.tensor_tensor(pad_row[:], iota_p[:], running[:], ALU.add))
            step(nc.vector.tensor_tensor(t_cmp[:], running[:].unsqueeze(2).to_broadcast([P, E, CAP // P]),
                                         iota_tile[:].unsqueeze(1).to_broadcast([P, E, CAP // P]), ALU.is_gt))
            step(nc.vector.tensor_reduce(n_tiles[:], t_cmp[:], AX.X, ALU.add))
            step(nc.vector.tensor_tensor(t_ee[:], n_tiles[:].unsqueeze(1).to_broadcast([P, E, E]), le_mask[:], ALU.mult))
            step(nc.vector.tensor_reduce(cum[:], t_ee[:], AX.X, ALU.add))
            step(nc.vector.tensor_tensor(cum_ex[:], cum[:], n_tiles[:], ALU.subtract))
            step(nc.vector.tensor_tensor(t_te[:], cum[:].unsqueeze(1).to_broadcast([P, NT, E]),
                                         iota_t[:].unsqueeze(2).to_broadcast([P, NT, E]), ALU.is_le))
            step(nc.vector.tensor_reduce(e_of[:], t_te[:], AX.X, ALU.add))
            step(nc.vector.tensor_tensor(t_tc[:], t_te[:], cum[:].unsqueeze(1).to_broadcast([P, NT, E]), ALU.mult))
            step(nc.vector.tensor_reduce(prev[:], t_tc[:], AX.X, ALU.max))
            step(nc.vector.tensor_tensor(within[:], iota_t[:], prev[:], ALU.subtract))
            step(nc.vector.tensor_scalar(within[:], within[:], float(P), None, ALU.mult))
            step(nc.vector.scalar_tensor_tensor(tile_row[:], e_of[:], float(STRIDE), within[:], ALU.mult, ALU.add))
            step(nc.vector.tensor_scalar(tile_expert[:], e_of[:], float(E - 1), None, ALU.min))
            choices = choice[:].rearrange("p b k -> p (b k)")
            step(nc.vector.tensor_tensor(t_be[:], choices.unsqueeze(2).to_broadcast([LQ, 2 * B, E]),
                                         iota_e[0:LQ, :].unsqueeze(1).to_broadcast([LQ, 2 * B, E]), ALU.is_equal))
            step(nc.vector.tensor_tensor(t_bc[:], t_be[:], cum_ex[0:LQ, :].unsqueeze(1).to_broadcast([LQ, 2 * B, E]), ALU.mult))
            step(nc.vector.tensor_reduce(first_tile[:], t_bc[:], AX.X, ALU.add))
            step(nc.vector.scalar_tensor_tensor(row_of[:].rearrange("p b k -> p (b k)"), first_tile[:], float(P),
                                                rank[:].rearrange("p b k -> p (b k)"), ALU.mult, ALU.add))
            assert done[0] == N_PLAN

            def lo_of_rows(t):
                dve.wait_ge(hT_hi, t + 1)
                nc.vector.tensor_tensor(hT_l[:].rearrange("p k n -> p (k n)"), hT_ps[:, 0:2 * P],
                                        hT_h[:].rearrange("p k n -> p (k n)").bitcast(F32), ALU.subtract).then_inc(hT_lo, 1)

            lo_of_rows(0)

            def tile(i, t, k):
                if there(t - 1, NT):
                    dve.wait_ge(hidT_made, t)
                    nc.vector.tensor_copy(hidT[:].rearrange("p j n -> p (j n)"), hidT_ps[:]).then_inc(hidT_done, 1)
                if there(t, NT):
                    dve.wait_ge(silu_done, t + 1)
                    dve.wait_ge(up_made, t + 1)
                    nc.vector.tensor_tensor(hid[:], up_ps[k][:], silu[:], ALU.mult).then_inc(hid_done, 1)
                if there(t + 1, NT):
                    lo_of_rows(t + 1)

            over_tiles(dve, tile)

            def last_pair(i):
                for s in range(2):
                    b = 2 * i + s
                    dve.wait_ge(gx_in[s], 16 * (i + 1))
                    dve.wait_ge(g_in[s], 32 * (i + 1))
                    w = row_at(share, b)
                    nc.vector.scalar_tensor_tensor(g_sum[:, s, :], g_rows[:, s, 0, :], w[:, 0:1], g_x[:, s, :],
                                                   ALU.mult, ALU.add).then_inc(gsum_done, 1)
                    dve.wait_ge(gsum_done, b + 1)
                    if not known(i) or i > 0:
                        dve.wait_ge(out_store[s], 16 * i)
                    nc.vector.scalar_tensor_tensor(g_out[:, s, :], g_rows[:, s, 1, :], w[:, 1:2], g_sum[:, s, :],
                                                   ALU.mult, ALU.add).then_inc(gout_done, 1)

            last_pair(0)
            with dve.Fori(1, NP) as i:
                last_pair(i)

        @block.tensor
        def _(pe):
            mm = nc.tensor.matmul

            def split_product(dst, pairs):
                todo = [(w, m) for wh, wl, mh, ml in pairs for w, m in ((wh, mh), (wh, ml), (wl, mh))]
                for n, (w, m) in enumerate(todo):
                    last = mm(dst, w, m, start=n == 0, stop=n == len(todo) - 1)
                return last

            def make(a, k, pair):
                odd, step, kind, arg = a.items[k]
                dst = A_ps[a.bank(k)]
                if not a.first or k >= 2:
                    if k >= 2:
                        if a.items[k - 2][2] == "V":
                            pe.wait_ge(v_done, a.values(k - 2))
                        else:
                            pe.wait_ge(lo_done, a.split(k - 2))
                    else:
                        pe.wait_ge(lo_done, a.split0 - 1 + k)
                slot = 1 - odd
                if kind == "yT":
                    slot = 0 if step < 0 else odd
                    pe.wait_ge(y_in[slot], 32 * (1 if a.first else pair + 2))
                    for t in range(KT):
                        last = nc.tensor.transpose(dst[:, t * KR:t * KR + KR], y_sb[:, slot, t, arg * P:arg * P + P],
                                                   ident[0:KR, 0:KR])
                elif kind == "xT":
                    pe.wait_ge(xn_done, 2 * (0 if a.first else pair + 1) + arg + 1)
                    for t in range(2):
                        last = nc.tensor.transpose(dst[:, t * LQ:t * LQ + LQ], xn[:, arg, t * P:t * P + P],
                                                   ident[0:LQ, 0:LQ])
                elif kind == "K":
                    if arg == 0:
                        pe.wait_ge(lo_done, context_split(a, odd))
                    c = slice(arg * P, arg * P + P)
                    last = product_ctx(dst[:, 0:LKE], c, slot, slice(0, LKE), True)
                elif kind == "q":
                    if arg == 0:
                        pe.wait_ge(lo_done, a.split(a.find(1, "xT", 1)))
                        if a.first:
                            pe.wait_ge(w_lo, 3)
                    c = slice(arg * P, arg * P + P)
                    last = split_product(dst[:, 0:2 * LQ], [(WqH[:, t, c], WqL[:, t, c], xT_h[:, t, :], xT_l[:, t, :])
                                                            for t in range(2)])
                else:
                    half, t = arg
                    if half:
                        slot = odd
                    c = slice(HD + half * 512, HD + half * 512 + 512)
                    last = product_ctx(dst[0:KR, :], c, slot, slice(t * KR, t * KR + KR), False)
                last.then_inc(made, 1)

            def product_ctx(dst, c, slot, rows, weights_stay):
                todo = [(WkvH[:, c], yA_h[:, slot, rows]), (WkvH[:, c], yA_l[:, slot, rows]),
                        (WkvL[:, c], yA_h[:, slot, rows]), (WkvT[:, c], yB[:, slot, rows]),
                        (WkvU[:, c], yB[0:CT, slot, rows])]
                for n, (w, y) in enumerate(todo):
                    last = mm(dst, w if weights_stay else y, y if weights_stay else w,
                              start=n == 0, stop=n == len(todo) - 1)
                return last

            def context_split(a, odd):
                if a.first:
                    return 2
                if odd:
                    return a.split(a.find(0, "yT", 1))
                return a.split_in_pair_before(1, "yT", 1)

            pe.wait_ge(consts, N_CONSTS)
            a = Ahead(None)
            for k in range(len(a.items)):
                if k == 4:
                    pe.wait_ge(w_lo, 2)
                make(a, k, None)

            def scores(a, i, odd, s, g):
                j, r = s // 2, s % 2
                if r == 0:
                    if odd:
                        pe.wait_ge(lo_done, a.split(a.find(0, "K", j)))
                    else:
                        pe.wait_ge(lo_done, a.split_in_pair_before(1, "q", j))
                if not known(g) or g >= 2:
                    pe.wait_ge(exp_done, g - 1)
                rows = slice(r * DK, r * DK + DK)
                q = slice(odd * LQ, odd * LQ + LQ)
                split_product(S_ps[r][0:LQ, 0:LKE], [(q_h[rows, j, q], q_l[rows, j, q], K_h[rows, j, :],
                                                      K_l[rows, j, :])]).then_inc(scores_made, 1)

            def turn_prob(i, odd, s, g):
                k, nth = (s - 1) % 2, 8 * (2 * i + odd) + (s - 1) // 2
                pe.wait_ge(exp_done, g + 1)
                if not known(g) or g >= 2:
                    pe.wait_ge(probT_odd if k else probT_even, nth)
                for t in range(KT):
                    last = nc.tensor.transpose(PT_ps[k][0:KR, t * LQ:t * LQ + LQ],
                                               prob[:, k, t * KR:t * KR + KR], ident[0:LQ, 0:LQ])
                last.then_inc(probT_made, 1)

            def weigh(a, i, odd, s, g):
                k, nth, head = s % 2, 8 * (2 * i + odd) + (s - 2) // 2, (s - 2) % H
                if head % HB == 0:
                    if not known(g) or g >= HB:
                        pe.wait_ge(O_done, 2 * (2 * i + odd) + head // HB)
                    if head:
                        pe.wait_ge(v_done, a.values(a.find(odd, "V", (1, KT - 1))))
                    elif odd:
                        pe.wait_ge(v_done, a.values(a.find(0, "V", (0, KT - 1))))
                    else:
                        pe.wait_ge(v_done, a.values_in_pair_before(1, "V", (0, KT - 1)))
                pe.wait_ge(probT_odd if k else probT_even, nth + 1)
                for t in range(KT):
                    last = mm(O_ps[0:LQ, head % HB * DK:head % HB * DK + DK], probT[:, k, t * LQ:t * LQ + LQ],
                              V[:, t, head * DK:head * DK + DK], start=t == 0, stop=t == KT - 1)
                last.then_inc(pv_made, 1)

            def turn_O(half):
                for j in range(4):
                    last = nc.tensor.transpose(C_ps[:, j * LQ:j * LQ + LQ],
                                               O_sb[:, (4 * half + j) * P:(4 * half + j) * P + P], ident[0:LQ, 0:LQ])
                last.then_inc(OT_made, 1)

            def after_attention(b, s, odd):
                if s == 1 and there(b - 2, B):
                    pe.wait_ge(chosen_done, b - 1)
                    pe.wait_ge(gates_done, b - 1)
                    mm(C_ps[0:LQ, 0:E], before[:], chosen[:], start=True, stop=True)
                    mm(C_ps[:, E:2 * E], ones[:], chosen[:], start=True, stop=True).then_inc(counts_made, 1)
                if s == 3 and there(b - 1, B):
                    pe.wait_ge(O_done, 2 * b)
                    if not known(b) or b >= 2:
                        pe.wait_ge(running_done, b - 1)
                    turn_O(1)
                if s == 5 and there(b - 1, B):
                    pe.wait_ge(OT_lo, 2 * b)
                    if known(b) and b == 1:
                        pe.wait_ge(w_lo, 4)
                    split_product(C_ps[0:LQ, 0:C], [(OT_h[:, j, :], OT_l[:, j, :], WpH[:, j, :], WpL[:, j, :])
                                                    for j in range(NJ)]).then_inc(proj_made, 1)
                if s == 8 and there(b - 1, B):
                    pe.wait_ge(x2_done, b)
                    pe.wait_ge(hn_done, b)
                    for t in range(2):
                        last = nc.tensor.transpose(C_ps[:, t * LQ:t * LQ + LQ], hn[:, 1 - odd, t * P:t * P + P],
                                                   ident[0:LQ, 0:LQ])
                    last.then_inc(hnT_made, 1)
                if s == 11 and there(b, B):
                    pe.wait_ge(O_done, 2 * b + 1)
                    if not known(b) or b >= 1:
                        pe.wait_ge(hnT_done, b)
                    turn_O(0)
                if s == 13 and there(b - 1, B):
                    pe.wait_ge(hnT_done, b)
                    if there(b, B):
                        pe.wait_ge(OT_lo, 2 * b + 1)
                    if known(b) and b == 1:
                        pe.wait_ge(small_in, 32)
                    for t in range(2):
                        last = mm(C_ps[0:LQ, 0:E], hnT[:, t, :], gw[:, t, :], start=t == 0, stop=t == 1)
                    last.then_inc(logits_made, 1)

            def pair(i):
                a = Ahead(i) if there(i, NP) else None
                for odd in (0, 1):
                    b = 2 * i + odd
                    for s in range(H):
                        g = H * b + s
                        if there(g, B * H):
                            scores(a, i, odd, s, g)
                        for k in (a.at(odd, s) if a else ()):
                            make(a, k, i)
                        if there(g - 1, B * H):
                            turn_prob(i, odd, s, g - 1)
                        after_attention(b, s, odd)
                        if there(g - 2, B * H):
                            weigh(a, i, odd, s, g - 2)

            over_pairs(pe, pair)

            pe.wait_ge(plan, N_PLAN)
            pe.wait_ge(running_done, B)

            def turn_rows(i, t, k):
                pe.wait_ge(h_in_ld[k], 16 * (i + 1))
                if not known(t) or t >= 1:
                    pe.wait_ge(hT_lo, t)
                for j in range(2):
                    last = nc.tensor.transpose(hT_ps[:, j * P:j * P + P], h_in[:, k, j * P:j * P + P], ident[:])
                last.then_inc(hT_made, 1)

            def expert_of(t):
                return pe.value_load(tile_expert[0:1, t:t + 1] if known(t) else tile_expert[0:1, bass.ds(t, 1)],
                                     min_val=0, max_val=E - 1)

            def hidden(dst, e, half):
                c = slice(half * FF, half * FF + FF)
                return split_product(dst, [(hT_h[:, j, :], hT_l[:, j, :], Wgu[:, e, 0, j, c], Wgu[:, e, 1, j, c])
                                           for j in range(2)])

            turn_rows(0, 0, 0)

            def tile(i, t, k):
                if there(t, NT):
                    e = expert_of(t)
                    pe.wait_ge(hT_lo, t + 1)
                    pe.wait_ge(wgu_lo, e + 1)
                    if not known(t) or t >= 2:
                        pe.wait_ge(silu_done, t - 1)
                    hidden(gate_ps[k][:], e, 0).then_inc(gate_made, 1)
                if there(t - 1, NT):
                    pe.wait_ge(hid_done, t)
                    if not known(t) or t >= 2:
                        pe.wait_ge(hidT_done, t - 1)
                    for j in range(FJ):
                        last = nc.tensor.transpose(hidT_ps[:, j * P:j * P + P], hid[:, j * P:j * P + P], ident[:])
                    last.then_inc(hidT_made, 1)
                if there(t, NT):
                    if not known(t) or t >= 2:
                        pe.wait_ge(hid_done, t - 1)
                    hidden(up_ps[k][:], e, 1).then_inc(up_made, 1)
                if there(t + 1, NT):
                    turn_rows(i + k, t + 1, 1 - k)
                if there(t - 1, NT):
                    e = expert_of(t - 1)
                    pe.wait_ge(hidT_done, t)
                    if known(t) and t == 1:
                        pe.wait_ge(wd_in, 16 * E)
                    if not known(t) or t >= 3:
                        pe.wait_ge(y_done, t - 2)
                    for j in range(FJ):
                        last = mm(down_ps[1 - k][:, 0:C], hidT[:, j, :], Wd[:, e, j, :], start=j == 0, stop=j == FJ - 1)
                    last.then_inc(down_made, 1)

            over_tiles(pe, tile)


_INS = ["x", "ctx_768", "L0_xattn_Wq", "L0_xattn_Wkv", "L0_xattn_Wproj", "L0_xattn_bproj",
        "L0_ffn_gate_w", "L0_ffn_gate_up_w", "L0_ffn_down_w"]


def kernel(**inputs):
    from concourse import bacc
    from concourse.bass_utils import run_bass_kernel_spmd

    nc = bacc.Bacc("TRN2", target_bir_lowering=False, num_devices=1)
    arrays, args = {}, []
    for name in _INS:
        a = np.ascontiguousarray(inputs[name])
        arrays[f"in_{name}"] = a
        args.append(nc.dram_tensor(f"in_{name}", a.shape, mybir.dt.from_np(a.dtype), kind="ExternalInput").ap())
    out = nc.dram_tensor("out", (B, LQ, C), F32, kind="ExternalOutput").ap()
    attention_and_experts(nc, *args, out)
    r = run_bass_kernel_spmd(nc, [arrays], core_ids=[0])
    return r.results[0]["out"]
```

```python
from contextlib import ExitStack

import numpy as np
import concourse.bass as bass
from concourse import mybir
from concourse.alu_op_type import AluOpType as ALU

F32 = mybir.dt.float32
F32R = mybir.dt.float32r
BF16 = mybir.dt.bfloat16
I32 = mybir.dt.int32
U32 = mybir.dt.uint32
ACT = mybir.ActivationFunctionType
AX = mybir.AxisListType

B, LQ, C = 32, 112, 256
LKV, CTX = 375, 192
H, DK = 16, 64
HD = H * DK
P = 128
NP = B // 2
KT, KR = 3, LKV // 3
LKE = LKV + 1
NJ = HD // P
HB = H // 2
CT = CTX - P
EPS = 1e-5
SCALE = DK ** -0.5

E, FF = 8, 512
TOK = B * LQ
CAP = TOK // P * P
assert CAP == TOK
STRIDE = CAP + P
NT = (2 * TOK + E * (P - 1)) // P
assert NT % 4 == 3
IDLE = NT - 2 * TOK // P
FJ = FF // P



def ahead(odd, step):
    out = []
    if step == 0 and odd:
        out += [("xT", 0), ("xT", 1)]
    if step % 2 == 1:
        out.append(("K", step // 2))
        if odd:
            out.append(("q", step // 2))
    if step in (2, 4, 6):
        out.append(("V", (1, step // 2 - 1)))
    if step in (10, 12, 14):
        out.append(("V", (0, step // 2 - 5)))
    if step == 8:
        out += [("yT", 0), ("yT", 1)]
    return [(odd, step, kind, a) for kind, a in out]


PAIR = [it for odd in (0, 1) for s in range(H) for it in ahead(odd, s)]
START = [(1, -1, "yT", 0), (1, -1, "yT", 1)] + [
    it for s in range(H) for it in ahead(1, s) if not (it[2] == "V" and it[3][0] == 1)]
LAST = [it for it in PAIR if it[2] not in ("q", "xT", "yT") and not (it[0] and it[2] == "K")
        and not (it[0] and it[2] == "V" and it[3][0] == 0)]


def n_split(items):
    return sum(it[2] != "V" for it in items)


class Ahead:

    def __init__(self, i):
        self.items = START if i is None else LAST if isinstance(i, int) and i == NP - 1 else PAIR
        k = 0 if i is None else i
        base = 0 if i is None else 1
        self.first = i is None
        self.n0 = base * len(START) + k * len(PAIR)
        self.split0 = base * n_split(START) + k * n_split(PAIR)
        self.v0 = base * (len(START) - n_split(START)) + k * (len(PAIR) - n_split(PAIR))
        self.bank0 = base * len(START) % 2

    def at(self, odd, step):
        return [k for k, it in enumerate(self.items) if it[0] == odd and it[1] == step]

    def find(self, odd, kind, a):
        return [k for k, it in enumerate(self.items) if (it[0], it[2], it[3]) == (odd, kind, a)][0]

    def bank(self, k):
        return (self.bank0 + k) % 2

    def made(self, k):
        return self.n0 + k + 1

    def split(self, k):
        return self.split0 + n_split(self.items[:k + 1])

    def values(self, k):
        return self.v0 + k + 1 - n_split(self.items[:k + 1])

    def split_in_pair_before(self, odd, kind, a):
        k = [n for n, it in enumerate(PAIR) if (it[0], it[2], it[3]) == (odd, kind, a)][0]
        return self.split0 - n_split(PAIR[k + 1:])

    def values_in_pair_before(self, odd, kind, a):
        k = [n for n, it in enumerate(PAIR) if (it[0], it[2], it[3]) == (odd, kind, a)][0]
        return self.v0 - (len(PAIR[k + 1:]) - n_split(PAIR[k + 1:]))


def known(v):
    return isinstance(v, int)


def there(v, end):
    return not known(v) or 0 <= v < end


def over_pairs(eng, body, first=1, end=NP - 1, tail=True):
    for i in range(first):
        body(i)
    with eng.Fori(first, end) as i:
        body(i)
    for i in range(end, NP):
        body(i)
    if tail:
        body(NP)


def over_tiles(body_of, eng):
    body_of(0)
    with eng.Fori(1, NT // 4) as i:
        body_of(i)
    body_of(NT // 4)


def row_at(t, b):
    return t[:, b, :] if known(b) else t[:, bass.ds(b, 1), :].rearrange("p o k -> p (o k)")


def dram_at(t, b):
    return t[b] if known(b) else t[bass.ds(b, 1)].rearrange("o q c -> (o q) c")


def attention_and_experts(nc, x, ctx_in, Wq, Wkv, Wproj, bproj, gate_w, gate_up_w, down_w, out):
    x2_dram = nc.dram_tensor("x2_scratch", [B, LQ, C], F32).ap()
    bins = nc.dram_tensor("bins", [E * STRIDE + IDLE * P, C], F32).ap()
    y_dram = nc.dram_tensor("expert_rows", [NT * P, C], F32).ap()

    with ExitStack() as stack:
        base = (nc.sbuf_base + 63) // 64 * 64
        size = (nc.sbuf_usable_end - base) // 64 * 64 - 64
        stack.enter_context(nc.sbuf_tensor("arena", [P, size // 4], F32))
        place = {"at": base + 64}

        def sb(name, shape, dt):
            bytes_ = int(np.prod(shape[1:])) * (2 if dt == BF16 else 4)
            t = nc.alloc_sbuf_tensor_at(name, shape, dt, offset=place["at"])
            place["at"] += (bytes_ + 31) // 32 * 32
            assert place["at"] <= base + size, name
            return t

        def sem(name):
            return stack.enter_context(nc.semaphore(name))

        ident = sb("ident", [P, P], F32)
        before = sb("before", [LQ, LQ], BF16)
        ones = sb("ones", [LQ, P], BF16)
        iota_e = sb("iota_e", [P, E], F32)
        le_mask = sb("le_mask", [P, E, E], F32)
        iota_tile = sb("iota_tile", [P, CAP // P], F32)
        iota_t = sb("iota_t", [P, NT], F32)
        iota_p = sb("iota_p", [P, E], F32)
        zero = sb("zero", [P, C], F32)
        running = sb("running", [P, E], F32)
        choice = sb("choice", [LQ, B, 2], F32)
        rank = sb("rank", [LQ, B, 2], F32)
        share = sb("share", [LQ, B, 2], F32)
        row_of = sb("row_of", [LQ, B, 2], I32)
        tile_row = sb("tile_row", [P, NT], I32)
        tile_expert = sb("tile_expert", [P, NT + 5], I32)
        row_now = sb("row_now", [LQ, 4, 2], I32)
        pad_row = sb("pad_row", [P, E], I32)
        wgu_at = place["at"]
        raw = sb("raw", [P, 2, 2 * 2 * FF], F32)
        shared_from = place["at"]

        WqH = sb("WqH", [P, 2, HD], F32R)
        WqL = sb("WqL", [P, 2, HD], F32R)
        WkvH = sb("WkvH", [P, 2 * HD], F32R)
        WkvL = sb("WkvL", [P, 2 * HD], F32R)
        WkvT = sb("WkvT", [P, 2 * HD], F32R)
        WkvU = sb("WkvU", [CT, 2 * HD], F32R)
        WpH = sb("WpH", [P, NJ, C], F32R)
        WpL = sb("WpL", [P, NJ, C], F32R)
        gw = sb("gw", [P, 2, E], F32)
        bias = sb("bias", [LQ, C], F32)
        y_sb = sb("y_sb", [KR, 2, KT, 2 * P], F32)
        yA_h = sb("yA_h", [P, 2, LKE], F32R)
        yA_l = sb("yA_l", [P, 2, LKE], F32R)
        yB = sb("yB", [P, 2, LKE], F32R)
        K_h = sb("K_h", [P, NJ, LKE], F32R)
        K_l = sb("K_l", [P, NJ, LKE], F32R)
        q_h = sb("q_h", [P, NJ, 2 * LQ], F32R)
        q_l = sb("q_l", [P, NJ, 2 * LQ], F32R)
        V = sb("V", [KR, KT, HD], F32)
        prob = sb("prob", [LQ, 2, LKV], F32)
        probT = sb("probT", [KR, 2, KT * LQ], F32)
        neg_max = sb("neg_max", [LQ, 2], F32)
        row_sum = sb("row_sum", [LQ, 2, HB], F32)
        inv_sum = sb("inv_sum", [LQ, HB], F32)
        O_sb = sb("O_sb", [LQ, HD], F32)
        OT_h = sb("OT_h", [P, NJ, LQ], F32R)
        OT_l = sb("OT_l", [P, NJ, LQ], F32R)
        x_sb = sb("x_sb", [LQ, 2, C], F32)
        xn = sb("xn", [LQ, 2, C], F32)
        xT_h = sb("xT_h", [P, 2, 2 * LQ], F32R)
        xT_l = sb("xT_l", [P, 2, 2 * LQ], F32R)
        stat1 = sb("stat1", [LQ, 2, 6], F32)
        mv1 = sb("mv1", [LQ, 2, 2], F32)
        std1 = sb("std1", [LQ, 2, 2], F32)
        x_res = sb("x_res", [LQ, 2, C], F32)
        x_bias = sb("x_bias", [LQ, 2, C], F32)
        x2 = sb("x2", [LQ, 2, C], F32)
        hn = sb("hn", [LQ, 2, C], F32)
        stat2 = sb("stat2", [LQ, 6], F32)
        mv2 = sb("mv2", [LQ, 2], F32)
        std2 = sb("std2", [LQ, 2], F32)
        minus_half = sb("minus_half", [LQ, 2], F32)
        hnT = sb("hnT", [P, 2, LQ], F32)
        neg_top = sb("neg_top", [LQ, 1], F32)
        gates = sb("gates", [LQ, E], F32)
        top = sb("top", [LQ, E], F32)
        top_i = sb("top_i", [LQ, E], U32)
        top_f = sb("top_f", [LQ, 2], F32)
        onehot = sb("onehot", [LQ, 2, E], F32)
        chosen = sb("chosen", [LQ, E], BF16)
        bin_at = sb("bin_at", [LQ, E], F32)
        picked = sb("picked", [LQ, 2, E], F32)
        rank2 = sb("rank2", [LQ, 2], F32)
        bin_row = sb("bin_row", [LQ, 2, 2], I32)
        top_sum = sb("top_sum", [LQ, 1], F32)
        inv_top = sb("inv_top", [LQ, 1], F32)

        part1_end = place["at"]
        wd_at = base + size - E * FJ * C * 4
        early = -(-(part1_end - wd_at) // (FJ * C * 4))
        place["at"] = wgu_at
        Wgu = sb("Wgu", [P, E, 2, 2, 2 * FF], F32R)
        h_in = sb("h_in", [P, 4, C], F32)
        hT_h = sb("hT_h", [P, 2, 2, P], F32R)
        hT_l = sb("hT_l", [P, 2, 2, P], F32R)
        silu = sb("silu", [P, FF], F32)
        hid = sb("hid", [P, FF], F32)
        hidT = sb("hidT", [P, FJ, P], F32)
        y_out = sb("y_out", [P, 2, C], F32)
        g_rows = sb("g_rows", [LQ, 4, 2, C], F32)
        g_x = sb("g_x", [LQ, 4, C], F32)
        g_sum = sb("g_sum", [LQ, 4, C], F32)
        g_out = sb("g_out", [LQ, 4, C], F32)
        assert place["at"] <= wd_at
        place["at"] = wd_at
        Wd = sb("Wd", [P, E, FJ, C], F32)
        place["at"] = shared_from
        t_cmp = sb("t_cmp", [P, E, CAP // P], F32)
        n_tiles = sb("n_tiles", [P, E], F32)
        t_ee = sb("t_ee", [P, E, E], F32)
        cum = sb("cum", [P, E], F32)
        cum_ex = sb("cum_ex", [P, E], F32)
        t_te = sb("t_te", [P, NT, E], F32)
        t_tc = sb("t_tc", [P, NT, E], F32)
        e_of = sb("e_of", [P, NT], F32)
        prev = sb("prev", [P, NT], F32)
        within = sb("within", [P, NT], F32)
        t_be = sb("t_be", [LQ, 2 * B, E], F32)
        t_bc = sb("t_bc", [LQ, 2 * B, E], F32)
        first_tile = sb("first_tile", [LQ, 2 * B], F32)

        banks = [stack.enter_context(nc.psum_tensor(f"bank{k}", [P, 512], F32)) for k in range(8)]
        S_ps, PT_ps, A_ps, O_ps, C_ps = banks[0:2], banks[2:4], banks[4:6], banks[6], banks[7]
        gate_ps, up_ps, hT_ps, hidT_ps = banks[0:2], banks[2:4], banks[4], banks[5]
        down_ps = banks[6:8]

        raw_in = [sem(f"raw_in{k}") for k in range(2)]
        small_in = sem("small_in")
        consts = sem("consts")
        passed = sem("passed")
        w_hi, w_lo = sem("w_hi"), sem("w_lo")
        y_in = [sem(f"y_in{k}") for k in range(2)]
        x_in = sem("x_in")
        xres_in = [sem(f"xres_in{k}") for k in range(2)]
        made = sem("made")
        hi_done, lo_done = sem("hi_done"), sem("lo_done")
        v_done = sem("v_done")
        scores_made, max_done, exp_done = sem("scores_made"), sem("max_done"), sem("exp_done")
        probT_made = sem("probT_made")
        probT_even, probT_odd = sem("probT_even"), sem("probT_odd")
        pv_made = sem("pv_made")
        inv_done, O_done = sem("inv_done"), sem("O_done")
        OT_made, OT_hi, OT_lo = sem("OT_made"), sem("OT_hi"), sem("OT_lo")
        proj_made, x2_done, x2_out = sem("proj_made"), sem("x2_done"), [sem("x2_out0"), sem("x2_out1")]
        st1, ag1, eps1, rs1, xn_done = sem("st1"), sem("ag1"), sem("eps1"), sem("rs1"), sem("xn_done")
        xb_done = sem("xb_done")
        st2, ag2, eps2, rs2, hn_done = sem("st2"), sem("ag2"), sem("eps2"), sem("rs2"), sem("hn_done")
        hnT_made, hnT_done = sem("hnT_made"), sem("hnT_done")
        logits_made, top_neg, gates_done = sem("logits_made"), sem("top_neg"), sem("gates_done")
        top_done, topi_done, topf_done = sem("top_done"), sem("topi_done"), sem("topf_done")
        onehot_done, chosen_done = sem("onehot_done"), sem("chosen_done")
        counts_made, binat_done, running_done = sem("counts_made"), sem("binat_done"), sem("running_done")
        picked_done, rank_done, row_done = sem("picked_done"), sem("rank_done"), sem("row_done")
        tsum_done, tinv_done = sem("tsum_done"), sem("tinv_done")
        kept = sem("kept")
        scattered = [sem("scattered0"), sem("scattered1")]
        idle_out, pads_out = sem("idle_out"), sem("pads_out")
        plan = sem("plan")
        wd_early, wd_in = sem("wd_early"), sem("wd_in")
        wgu_raw = [sem(f"wgu_raw{e}") for e in range(E)]
        wgu_hi, wgu_lo = sem("wgu_hi"), sem("wgu_lo")
        h_in_ld = [sem(f"h_in{k}") for k in range(4)]
        hT_made, hT_hi, hT_lo = sem("hT_made"), sem("hT_hi"), sem("hT_lo")
        gate_made, up_made, silu_done, hid_done = sem("gate_made"), sem("up_made"), sem("silu_done"), sem("hid_done")
        hidT_made, hidT_done, down_made, y_done = sem("hidT_made"), sem("hidT_done"), sem("down_made"), sem("y_done")
        y_store = [sem("y_store0"), sem("y_store1")]
        g_in = [sem(f"g_in{k}") for k in range(4)]
        gx_in = [sem(f"gx_in{k}") for k in range(4)]
        row_ready = sem("row_ready")
        gsum_done, gout_done = sem("gsum_done"), sem("gout_done")
        out_store = [sem(f"out_store{k}") for k in range(4)]

        N_CONSTS = 18
        N_PLAN = 18
        block = stack.enter_context(nc.Block())

        @block.sync
        def _(sp):
            def load_y(b, slot):
                rows = ctx_in[b:b + 1] if known(b) else ctx_in[bass.ds(b, 1)]
                rows = rows.rearrange("o (k p) c -> p (o k) c", p=KR)
                sp.dma_start(y_sb[:, slot, :, 0:CTX], rows).then_inc(y_in[slot], 16)
                sp.dma_start(y_sb[:, slot, :, CTX:2 * P], rows[:, :, P:CTX]).then_inc(y_in[slot], 16)

            def load_x(pair):
                rows = x[bass.ds(2 * pair, 2)] if not known(pair) else x[2 * pair:2 * pair + 2]
                sp.dma_start(x_sb[:], rows.rearrange("b q c -> q b c")).then_inc(x_in, 16)

            sp.sem_inc(x2_out[1], 16)
            load_y(0, 0)
            sp.dma_start(raw[:, 0, :], Wkv[0:P, :]).then_inc(raw_in[0], 16)
            load_x(0)
            sp.dma_start(raw[0:CT, 1, :], Wkv[P:CTX, :]).then_inc(raw_in[1], 16)
            sp.dma_start(raw[CT:P, 1, :], Wkv[P:CTX, :]).then_inc(raw_in[1], 16)
            load_y(1, 1)
            sp.dma_start(gw[:], gate_w.rearrange("(k p) e -> p k e", p=P)).then_inc(small_in, 16)
            sp.dma_start(bias[:], bproj.rearrange("(o c) -> o c", o=1).to_broadcast([LQ, C])).then_inc(small_in, 16)
            sp.wait_ge(w_lo, 1)
            sp.dma_start(raw[:, 0, :], Wq.rearrange("(k p) n -> p k n", p=P)).then_inc(raw_in[0], 16)
            sp.wait_ge(w_lo, 2)
            sp.dma_start(raw[:, 1, :], Wproj.rearrange("(k p) n -> p k n", p=P)).then_inc(raw_in[1], 16)
            a = Ahead(None)
            sp.wait_ge(made, a.made(1))
            load_y(2, 0)
            sp.wait_ge(xn_done, 2)
            load_x(1)
            sp.wait_ge(made, a.made([k for k, it in enumerate(START) if it[2:] == ("yT", 1)][1]))
            load_y(3, 1)
            sp.wait_ge(consts, 1)
            for k in range(IDLE):
                r = E * STRIDE + k * P
                sp.dma_start(bins[r:r + P, :], zero[:]).then_inc(idle_out, 16)

            def pair(i):
                a = Ahead(i)
                if known(i) and i == NP - 2:
                    sp.wait_ge(w_lo, 4)
                    sp.dma_start(Wgu[:, 0, 1].bitcast(F32),
                                 gate_up_w[0].rearrange("(k p) n -> p k n", p=P)).then_inc(wgu_raw[0], 16)
                    sp.dma_start(Wd[:, early:E].rearrange("p e k n -> p (e k) n"),
                                 down_w[early:E].rearrange("e (k p) n -> p (e k) n", p=P)).then_inc(wd_early, 16)
                for odd in (0, 1):
                    b = 2 * i + odd
                    if there(b, B):
                        if not known(b) or b >= 2:
                            sp.wait_ge(xb_done, b - 1)
                        sp.dma_start(x_res[:, odd, :], dram_at(x, b)).then_inc(xres_in[odd], 16)
                    if there(b - 1, B):
                        sp.wait_ge(x2_done, b)
                        sp.dma_start(dram_at(x2_dram, b - 1), x2[:, 1 - odd, :]).then_inc(x2_out[1 - odd], 16)
                    if not known(i) or i + 2 < NP:
                        sp.wait_ge(made, a.made(a.find(odd, "yT", 1)))
                        load_y(b + 4, odd)
                    if odd and (not known(i) or i + 2 < NP):
                        sp.wait_ge(xn_done, 2 * (i + 2))
                        load_x(i + 2)

            over_pairs(sp, pair, 1, NP - 2)

            sp.wait_ge(plan, N_PLAN)
            sp.wait_ge(counts_made, B)
            sp.wait_ge(gates_done, B)
            sp.wait_ge(x2_out[0], 16 * NP)
            sp.wait_ge(x2_out[1], 16 * NP + 16)
            sp.wait_ge(scattered[0], 32 * NP)
            sp.wait_ge(scattered[1], 32 * NP)
            sp.wait_ge(pads_out, 16 * E)
            sp.wait_ge(idle_out, 16 * IDLE)

            def load_rows(t, slot):
                r = sp.value_load(tile_row[0:1, t:t + 1] if known(t) else tile_row[0:1, bass.ds(t, 1)],
                                  min_val=0, max_val=E * STRIDE + (IDLE - 1) * P)
                sp.dma_start(h_in[:, slot, :], bins[bass.ds(r, P), :]).then_inc(h_in_ld[slot], 16)

            def load_x2(b, slot):
                sp.dma_start(g_x[:, slot, :], dram_at(x2_dram, b)).then_inc(gx_in[slot], 16)

            for t in range(3):
                load_rows(t, t)
            for b in range(4):
                load_x2(b, b)

            def four_tiles(i):
                for k in range(4):
                    t = 4 * i + k
                    if there(t + 3, NT):
                        if not known(t) or t >= 1:
                            sp.wait_ge(hT_made, t)
                        load_rows(t + 3, (k + 3) % 4)
                    if there(t - 1, NT):
                        sp.wait_ge(y_done, t)
                        rows = y_dram[(t - 1) * P:t * P, :] if known(t) else y_dram[bass.ds(t * P - P, P), :]
                        sp.dma_start(rows, y_out[:, (k + 1) % 2, :]).then_inc(y_store[(k + 1) % 2], 16)

            over_tiles(four_tiles, sp)

            def last_four(i):
                for k in range(4):
                    b = 4 * i + k
                    sp.wait_ge(gout_done, b + 1)
                    sp.dma_start(dram_at(out, b), g_out[:, k, :]).then_inc(out_store[k], 16)
                    if not known(i) or i < B // 4 - 1:
                        load_x2(b + 4, k)

            with sp.Fori(0, B // 4 - 1) as i:
                last_four(i)
            last_four(B // 4 - 1)
            for k in range(4):
                sp.wait_ge(out_store[k], 16 * (B // 4))

        @block.gpsimd
        def _(pool):
            pool.memset(zero[:], 0.0).then_inc(consts, 1)
            pool.memset(ident[:], 0.0).then_inc(consts, 1)
            pool.memset(before[:], 1.0).then_inc(consts, 1)
            pool.memset(ones[:], 1.0).then_inc(consts, 1)
            pool.memset(le_mask[:], 1.0).then_inc(consts, 1)
            pool.memset(minus_half[:], -0.5).then_inc(consts, 1)
            pool.memset(running[:], 0.0).then_inc(consts, 1)
            pool.memset(tile_expert[:], 0).then_inc(consts, 1)
            for t in (yA_h, yA_l, yB):
                pool.memset(t[:, :, LKV:LKE].bitcast(F32), 0.0).then_inc(consts, 1)
            pool.iota(iota_e[:], [[1, E]], base=0, channel_multiplier=0,
                      allow_small_or_imprecise_dtypes=True).then_inc(consts, 1)
            pool.iota(iota_tile[:], [[P, CAP // P]], base=0, channel_multiplier=0,
                      allow_small_or_imprecise_dtypes=True).then_inc(consts, 1)
            pool.iota(iota_t[:], [[1, NT]], base=0, channel_multiplier=0,
                      allow_small_or_imprecise_dtypes=True).then_inc(consts, 1)
            pool.iota(iota_p[:], [[STRIDE, E]], base=0, channel_multiplier=1,
                      allow_small_or_imprecise_dtypes=True).then_inc(consts, 1)
            pool.wait_ge(consts, N_CONSTS - 3)
            pool.affine_select(out=ident[:], in_=ident[:], compare_op=ALU.not_equal, fill=1.0, base=0,
                               pattern=[[-1, P]], channel_multiplier=1).then_inc(consts, 1)
            pool.affine_select(out=before[:], in_=before[:], compare_op=ALU.is_gt, fill=0.0, base=0,
                               pattern=[[1, LQ]], channel_multiplier=-1).then_inc(consts, 1)
            pool.affine_select(out=le_mask[:], in_=le_mask[:], compare_op=ALU.is_ge, fill=0.0, base=0,
                               pattern=[[1, E], [-1, E]], channel_multiplier=0).then_inc(consts, 1)

            def norm_x(pair):
                pool.wait_ge(ag1, 2 * pair + 2)
                pool.sem_inc(passed, 1)
                pool.tensor_scalar(std1[:, :, 0], mv1[:, :, 1], EPS, None, ALU.add).then_inc(eps1, 1)
                pool.wait_ge(eps1, pair + 1)
                pool.tensor_tensor(std1[:, :, 1], std1[:, :, 0], minus_half[:, 0:2], ALU.pow).then_inc(rs1, 1)
                if not known(pair) or pair > 0:
                    a = Ahead(pair - 2 if not known(pair) or pair > 1 else None)
                    pool.wait_ge(made, a.made(a.find(1, "xT", 1)))
                pool.wait_ge(rs1, pair + 1)
                pool.sem_inc(passed, 1)
                for r in range(2):
                    pool.tensor_scalar(xn[:, r, :], x_sb[:, r, :], mv1[:, r, 0:1], std1[:, r, 1:2],
                                       ALU.subtract, ALU.mult).then_inc(xn_done, 1)

            norm_x(0)

            def scatter(b, slot):
                pool.wait_ge(row_done, b + 1)
                pool.sem_inc(passed, 1)
                for k in range(2):
                    pool.indirect_dma_start(bins, bass.IndirectOffsetOnAxis(ap=bin_row[:, slot, k:k + 1], axis=0),
                                            hn[:, slot, :], None).then_inc(scattered[slot], 16)

            def split_expert(e):
                pool.wait_ge(wgu_raw[e], 16)
                pool.tensor_copy(Wgu[:, e, 0], Wgu[:, e, 1].bitcast(F32)).then_inc(wgu_hi, 1)
                pool.wait_ge(wgu_hi, e + 1)
                pool.tensor_tensor(Wgu[:, e, 1], Wgu[:, e, 1].bitcast(F32), Wgu[:, e, 0].bitcast(F32),
                                   ALU.subtract).then_inc(wgu_lo, 1)

            def pair(i):
                for odd in (0, 1):
                    b = 2 * i + odd
                    if there(b, B):
                        pool.wait_ge(xres_in[odd], 16 * (i + 1))
                        if known(b) and b == 0:
                            pool.wait_ge(small_in, 32)
                        if not known(b) or b >= 2:
                            pool.wait_ge(x2_done, b - 1)
                        pool.tensor_tensor(x_bias[:, odd, :], x_res[:, odd, :], bias[:], ALU.add).then_inc(xb_done, 1)
                    if there(b - 2, B):
                        scatter(b - 2, odd)
                    if there(b - 1, B):
                        pool.wait_ge(ag2, b)
                        pool.sem_inc(passed, 1)
                        pool.tensor_scalar(std2[:, 0:1], mv2[:, 1:2], EPS, None, ALU.add).then_inc(eps2, 1)
                        pool.wait_ge(eps2, b)
                        pool.tensor_tensor(std2[:, 1:2], std2[:, 0:1], minus_half[:, 0:1], ALU.pow).then_inc(rs2, 1)
                        if not known(b) or b >= 3:
                            pool.wait_ge(scattered[1 - odd], 32 * (i - 1 + odd))
                        pool.wait_ge(rs2, b)
                        pool.sem_inc(passed, 1)
                        pool.tensor_scalar(hn[:, 1 - odd, :], x2[:, 1 - odd, :], mv2[:, 0:1], std2[:, 1:2],
                                           ALU.subtract, ALU.mult).then_inc(hn_done, 1)
                    if not odd and (not known(i) or i + 1 < NP):
                        norm_x(i + 1)
                    if known(i) and i == NP - 1 and not odd:
                        split_expert(0)

            over_pairs(pool, pair, 2)

            pool.wait_ge(plan, 1)
            for e in range(E):
                pool.indirect_dma_start(bins, bass.IndirectOffsetOnAxis(ap=pad_row[:, e:e + 1], axis=0),
                                        zero[:], None).then_inc(pads_out, 16)

            for e in range(1, E):
                split_expert(e)

            for k in range(2):
                pool.wait_ge(y_store[k], 16 * ((NT + 1 - k) // 2))

            def last_four(i):
                for s in range(4):
                    b = 4 * i + s
                    if not known(i) or i > 0:
                        pool.wait_ge(g_in[s], 32 * i)
                        pool.wait_ge(gout_done, b - 3)
                    pool.tensor_copy(row_now[:, s, :], row_at(row_of, b)).then_inc(row_ready, 1)
                    pool.wait_ge(row_ready, b + 1)
                    pool.sem_inc(passed, 1)
                    for k in range(2):
                        pool.indirect_dma_start(g_rows[:, s, k, :], None, y_dram,
                                                bass.IndirectOffsetOnAxis(ap=row_now[:, s, k:k + 1], axis=0)).then_inc(g_in[s], 16)

            last_four(0)
            with pool.Fori(1, B // 4) as i:
                last_four(i)

        @block.scalar
        def _(act):
            def hi_of_weight(dst, slot, loads, scale=1.0):
                act.wait_ge(raw_in[slot], 16 * loads)
                nc.scalar.mul(dst, raw[:, slot, :], scale).then_inc(w_hi, 1)

            def evacuate(a, k):
                odd, step, kind, arg = a.items[k]
                src = A_ps[a.bank(k)]
                act.wait_ge(made, a.made(k))
                if kind == "V":
                    half, t = arg
                    nc.scalar.copy(V[:, t, half * 512:half * 512 + 512], src[0:KR, :]).then_inc(v_done, 1)
                elif kind == "K":
                    nc.scalar.copy(K_h[:, arg, :], src[:, 0:LKE]).then_inc(hi_done, 1)
                elif kind == "q":
                    nc.scalar.copy(q_h[:, arg, :], src[:, 0:2 * LQ]).then_inc(hi_done, 1)
                elif kind == "yT":
                    slot = 0 if step < 0 else odd
                    dst = (yA_h if arg == 0 else yB)[:, slot, 0:LKV]
                    nc.scalar.copy(dst, src[:, 0:LKV]).then_inc(hi_done, 1)
                else:
                    nc.scalar.copy(xT_h[:, :, arg * LQ:arg * LQ + LQ],
                                   src[:, 0:2 * LQ].rearrange("p (k q) -> p k q", k=2)).then_inc(hi_done, 1)

            a = Ahead(None)
            evacuate(a, 0)
            evacuate(a, 1)
            hi_of_weight(WkvH[:], 0, 1)
            hi_of_weight(WkvT[:], 1, 2)
            evacuate(a, 2)
            evacuate(a, 3)
            hi_of_weight(WqH[:].rearrange("p k n -> p (k n)"), 0, 2, SCALE)
            for k in range(4, len(a.items)):
                evacuate(a, k)
            hi_of_weight(WpH[:].rearrange("p k n -> p (k n)"), 1, 3)

            def pair(i):
                a = Ahead(i) if there(i, NP) else None
                for odd in (0, 1):
                    b = 2 * i + odd
                    for s in range(H):
                        g = H * b + s
                        items = a.at(odd, s) if a else []
                        short = items[:1] if s in (0, 8) else []
                        for k in short:
                            evacuate(a, k)
                        if there(g, B * H):
                            act.wait_ge(max_done, g + 1)
                            if not known(g) or g >= 2:
                                act.wait_ge(probT_made, g - 1)
                            nc.scalar.activation(prob[:, s % 2, :], S_ps[s % 2][0:LQ, 0:LKV], ACT.Exp,
                                                 bias=neg_max[:, s % 2:s % 2 + 1],
                                                 accum_out=row_sum[:, s // HB, s % HB:s % HB + 1]).then_inc(exp_done, 1)
                        for k in items[len(short):1]:
                            evacuate(a, k)
                        if s % 2 == 1 and there(g - 1, B * H):
                            act.wait_ge(probT_made, g)
                            if not known(g) or g >= 3:
                                act.wait_ge(pv_made, g - 2)
                            nc.scalar.copy(probT[:, 0, :], PT_ps[0][0:KR, 0:KT * LQ]).then_inc(probT_even, 1)
                        if s in (3, 11) and there(b - (s == 3), B):
                            half = s == 3
                            n = 2 * (b - half) + half
                            act.wait_ge(OT_made, n + 1)
                            nc.scalar.copy(OT_h[:, 4 * half:4 * half + 4, :].rearrange("p j q -> p (j q)"),
                                           C_ps[:, 0:4 * LQ]).then_inc(OT_hi, 1)
                        for k in items[1:]:
                            evacuate(a, k)
                        if s == 13 and there(b - 1, B):
                            act.wait_ge(top_neg, b)
                            nc.scalar.activation(gates[:], C_ps[0:LQ, 0:E], ACT.Exp,
                                                 bias=neg_top[:, 0:1]).then_inc(gates_done, 1)

            over_pairs(act, pair)

            act.wait_ge(plan, N_PLAN)
            act.wait_ge(counts_made, B)
            act.wait_ge(x2_out[0], 16 * NP)
            act.wait_ge(x2_out[1], 16 * NP + 16)
            act.wait_ge(scattered[0], 32 * NP)
            act.wait_ge(scattered[1], 32 * NP)
            act.wait_ge(h_in_ld[2], 16)
            act.dma_start(Wd[:, 0:early].rearrange("p e k n -> p (e k) n"),
                          down_w[0:early].rearrange("e (k p) n -> p (e k) n", p=P)).then_inc(wd_in, 16)
            for e in range(1, E):
                act.dma_start(Wgu[:, e, 1].bitcast(F32),
                              gate_up_w[e].rearrange("(k p) n -> p k n", p=P)).then_inc(wgu_raw[e], 16)

            def hi_of_rows(t, slot):
                act.wait_ge(hT_made, t + 1)
                nc.scalar.copy(hT_h[:, slot].rearrange("p k n -> p (k n)"), hT_ps[:, 0:2 * P]).then_inc(hT_hi, 1)

            hi_of_rows(0, 0)

            def four_tiles(i):
                for k in range(4):
                    t = 4 * i + k
                    if there(t, NT):
                        act.wait_ge(gate_made, t + 1)
                        if not known(t) or t >= 1:
                            act.wait_ge(hid_done, t)
                        nc.scalar.activation(silu[:], gate_ps[k % 2][:], ACT.Silu).then_inc(silu_done, 1)
                    if there(t + 1, NT):
                        hi_of_rows(t + 1, (k + 1) % 2)
                    if there(t - 1, NT):
                        act.wait_ge(down_made, t)
                        if not known(t) or t >= 3:
                            act.wait_ge(y_store[(k + 1) % 2], 16 * (2 * i + (k - 1) // 2))
                        nc.scalar.copy(y_out[:, (k + 1) % 2, :], down_ps[(k + 1) % 2][:, 0:C]).then_inc(y_done, 1)

            over_tiles(four_tiles, act)

        @block.vector
        def _(dve):
            def norm_x(pair):
                dve.wait_ge(x_in, 16 * (pair + 1))
                if not known(pair) or pair > 0:
                    dve.wait_ge(xn_done, 2 * pair)
                for r in range(2):
                    nc.vector.bn_stats(stat1[:, r, :], x_sb[:, r, :]).then_inc(st1, 1)
                for r in range(2):
                    dve.wait_ge(st1, 2 * pair + 1 + r)
                    dve.sem_inc(passed, 1)
                    nc.vector.bn_aggr(mv1[:, r, :], stat1[:, r, :]).then_inc(ag1, 1)

            def low_part(a, k):
                odd, step, kind, arg = a.items[k]
                if kind == "V":
                    return
                src = A_ps[a.bank(k)]
                dve.wait_ge(hi_done, a.split(k))
                if kind == "K":
                    lo, ps, hi = K_l[:, arg, :], src[:, 0:LKE], K_h[:, arg, :]
                elif kind == "q":
                    lo, ps, hi = q_l[:, arg, :], src[:, 0:2 * LQ], q_h[:, arg, :]
                elif kind == "yT":
                    slot = 0 if step < 0 else odd
                    if arg == 0:
                        lo, ps, hi = yA_l[:, slot, 0:LKV], src[:, 0:LKV], yA_h[:, slot, 0:LKV]
                    else:
                        lo, ps, hi = yB[CT:P, slot, 0:LKV], src[CT:P, 0:LKV], yB[CT:P, slot, 0:LKV]
                else:
                    lo, hi = xT_l[:, :, arg * LQ:arg * LQ + LQ], xT_h[:, :, arg * LQ:arg * LQ + LQ]
                    ps = src[:, 0:2 * LQ].rearrange("p (k q) -> p k q", k=2)
                nc.vector.tensor_tensor(lo, ps, hi.bitcast(F32), ALU.subtract).then_inc(lo_done, 1)

            a = Ahead(None)
            low_part(a, 0)
            low_part(a, 1)
            norm_x(0)
            dve.wait_ge(w_hi, 1)
            nc.vector.tensor_tensor(WkvL[:], raw[:, 0, :], WkvH[:].bitcast(F32), ALU.subtract).then_inc(w_lo, 1)
            dve.wait_ge(w_hi, 2)
            nc.vector.tensor_tensor(WkvU[:], raw[0:CT, 1, :], WkvT[0:CT, :].bitcast(F32), ALU.subtract).then_inc(w_lo, 1)
            low_part(a, 2)
            low_part(a, 3)
            dve.wait_ge(w_hi, 3)
            nc.vector.scalar_tensor_tensor(WqL[:].rearrange("p k n -> p (k n)"), raw[:, 0, :], SCALE,
                                           WqH[:].rearrange("p k n -> p (k n)").bitcast(F32),
                                           ALU.mult, ALU.subtract).then_inc(w_lo, 1)
            for k in range(4, len(a.items)):
                low_part(a, k)
            dve.wait_ge(w_hi, 4)
            nc.vector.tensor_tensor(WpL[:].rearrange("p k n -> p (k n)"), raw[:, 1, :],
                                    WpH[:].rearrange("p k n -> p (k n)").bitcast(F32), ALU.subtract).then_inc(w_lo, 1)

            def invert_sums(n, k):
                dve.wait_ge(exp_done, HB * n + HB)
                nc.vector.reciprocal(inv_sum[:], row_sum[:, k, :]).then_inc(inv_done, 1)

            def normalise(n, k):
                dve.wait_ge(inv_done, n + 1)
                dve.wait_ge(pv_made, HB * n + HB)
                nc.vector.tensor_tensor(O_sb[:, k * 512:k * 512 + 512].rearrange("p (h d) -> p h d", h=HB),
                                        O_ps[0:LQ, :].rearrange("p (h d) -> p h d", h=HB),
                                        inv_sum[:].unsqueeze(2).to_broadcast([LQ, HB, DK]),
                                        ALU.mult).then_inc(O_done, 1)

            def residual(i, b, slot):
                dve.wait_ge(proj_made, b + 1)
                dve.wait_ge(xb_done, b + 1)
                if not known(b) or b >= 2:
                    dve.wait_ge(x2_out[slot], 16 * i)
                nc.vector.tensor_tensor(x2[:, slot, :], C_ps[0:LQ, 0:C], x_bias[:, slot, :], ALU.add).then_inc(x2_done, 1)
                dve.wait_ge(x2_done, b + 1)
                nc.vector.bn_stats(stat2[:], x2[:, slot, :]).then_inc(st2, 1)
                dve.wait_ge(st2, b + 1)
                dve.sem_inc(passed, 1)
                nc.vector.bn_aggr(mv2[:], stat2[:]).then_inc(ag2, 1)

            def choose(b):
                dve.wait_ge(gates_done, b + 1)
                dve.sem_inc(passed, 1)
                nc.vector.max(top[:], gates[:]).then_inc(top_done, 1)
                dve.wait_ge(top_done, b + 1)
                dve.sem_inc(passed, 1)
                nc.vector.max_index(top_i[:], top[:], gates[:]).then_inc(topi_done, 1)

            def mark(b):
                dve.wait_ge(topi_done, b + 1)
                nc.vector.tensor_copy(top_f[:], top_i[:, 0:2]).then_inc(topf_done, 1)
                nc.vector.tensor_reduce(top_sum[:], top[:, 0:2], AX.X, ALU.add).then_inc(tsum_done, 1)
                dve.wait_ge(topf_done, b + 1)
                nc.vector.tensor_tensor(onehot[:], iota_e[0:LQ, :].unsqueeze(1).to_broadcast([LQ, 2, E]),
                                        top_f[:].unsqueeze(2).to_broadcast([LQ, 2, E]),
                                        ALU.is_equal).then_inc(onehot_done, 1)
                dve.wait_ge(tsum_done, b + 1)
                nc.vector.reciprocal(inv_top[:], top_sum[:]).then_inc(tinv_done, 1)
                dve.wait_ge(onehot_done, b + 1)
                nc.vector.tensor_tensor(chosen[:], onehot[:, 0, :], onehot[:, 1, :], ALU.add).then_inc(chosen_done, 1)
                dve.wait_ge(tinv_done, b + 1)
                nc.vector.tensor_scalar(row_at(share, b), top[:, 0:2], inv_top[:, 0:1], None, ALU.mult).then_inc(kept, 1)

            def assign(b, slot):
                dve.wait_ge(counts_made, b + 1)
                nc.vector.tensor_tensor(bin_at[:], C_ps[0:LQ, 0:E], running[0:LQ, :], ALU.add).then_inc(binat_done, 1)
                dve.wait_ge(binat_done, b + 1)
                nc.vector.tensor_tensor(running[:], C_ps[:, E:2 * E], running[:], ALU.add).then_inc(running_done, 1)
                nc.vector.tensor_tensor(picked[:], onehot[:], bin_at[:].unsqueeze(1).to_broadcast([LQ, 2, E]),
                                        ALU.mult).then_inc(picked_done, 1)
                dve.wait_ge(picked_done, b + 1)
                nc.vector.tensor_reduce(rank2[:], picked[:], AX.X, ALU.add).then_inc(rank_done, 1)
                dve.wait_ge(rank_done, b + 1)
                nc.vector.scalar_tensor_tensor(bin_row[:, slot, :], top_f[:], float(STRIDE), rank2[:],
                                               ALU.mult, ALU.add).then_inc(row_done, 1)
                nc.vector.tensor_copy(row_at(rank, b), rank2[:]).then_inc(kept, 1)
                nc.vector.tensor_copy(row_at(choice, b), top_f[:]).then_inc(kept, 1)

            def pair(i):
                a = Ahead(i) if there(i, NP) else None
                for odd in (0, 1):
                    b = 2 * i + odd
                    for s in range(H):
                        g = H * b + s
                        if s == 2 and there(b - 1, B):
                            normalise(2 * b - 1, 1)
                        if s == 10 and there(b, B):
                            normalise(2 * b, 0)
                        if there(g, B * H):
                            dve.wait_ge(scores_made, g + 1)
                            nc.vector.tensor_reduce(neg_max[:, s % 2:s % 2 + 1], S_ps[s % 2][0:LQ, 0:LKV],
                                                    AX.X, ALU.max, negate=True).then_inc(max_done, 1)
                        if s == 15 and there(b - 1, B):
                            mark(b - 1)
                        if s == 1 and there(b - 1, B):
                            invert_sums(2 * b - 1, 1)
                        if s == 9 and there(b, B):
                            invert_sums(2 * b, 0)
                        if s == 1 and there(b - 2, B):
                            assign(b - 2, odd)
                        items = a.at(odd, s) if a else []
                        for k in items[:1]:
                            low_part(a, k)
                        if s % 2 == 0 and there(g - 1, B * H):
                            dve.wait_ge(probT_made, g)
                            if not known(g) or g >= 3:
                                dve.wait_ge(pv_made, g - 2)
                            nc.vector.tensor_copy(probT[:, 1, :], PT_ps[1][0:KR, 0:KT * LQ]).then_inc(probT_odd, 1)
                        if s in (3, 11) and there(b - (s == 3), B):
                            half = int(s == 3)
                            dve.wait_ge(OT_hi, 2 * (b - half) + half + 1)
                            nc.vector.tensor_tensor(OT_l[:, 4 * half:4 * half + 4, :].rearrange("p j q -> p (j q)"),
                                                    C_ps[:, 0:4 * LQ],
                                                    OT_h[:, 4 * half:4 * half + 4, :].rearrange("p j q -> p (j q)").bitcast(F32),
                                                    ALU.subtract).then_inc(OT_lo, 1)
                        if s == 5 and there(b - 1, B):
                            residual(i, b - 1, 1 - odd)
                        if s == 8 and there(b - 1, B):
                            dve.wait_ge(hnT_made, b)
                            nc.vector.tensor_copy(hnT[:].rearrange("p k q -> p (k q)"), C_ps[:, 0:2 * LQ]).then_inc(hnT_done, 1)
                        if s == 12 and not odd and (not known(i) or i + 1 < NP):
                            norm_x(i + 1)
                        if there(b - 1, B):
                            if s == 13:
                                dve.wait_ge(logits_made, b)
                                nc.vector.tensor_reduce(neg_top[:], C_ps[0:LQ, 0:E], AX.X, ALU.max,
                                                        negate=True).then_inc(top_neg, 1)
                            if s == 14:
                                choose(b - 1)
                        for k in items[1:]:
                            low_part(a, k)

            over_pairs(dve, pair)

            done = [0]

            def step(ins):
                done[0] += 1
                ins.then_inc(plan, 1)
                dve.wait_ge(plan, done[0])

            dve.wait_ge(running_done, B)
            dve.wait_ge(kept, 3 * B)
            step(nc.vector.tensor_tensor(pad_row[:], iota_p[:], running[:], ALU.add))
            step(nc.vector.tensor_tensor(t_cmp[:], running[:].unsqueeze(2).to_broadcast([P, E, CAP // P]),
                                         iota_tile[:].unsqueeze(1).to_broadcast([P, E, CAP // P]), ALU.is_gt))
            step(nc.vector.tensor_reduce(n_tiles[:], t_cmp[:], AX.X, ALU.add))
            step(nc.vector.tensor_tensor(t_ee[:], n_tiles[:].unsqueeze(1).to_broadcast([P, E, E]), le_mask[:], ALU.mult))
            step(nc.vector.tensor_reduce(cum[:], t_ee[:], AX.X, ALU.add))
            step(nc.vector.tensor_tensor(cum_ex[:], cum[:], n_tiles[:], ALU.subtract))
            step(nc.vector.tensor_tensor(t_te[:], cum[:].unsqueeze(1).to_broadcast([P, NT, E]),
                                         iota_t[:].unsqueeze(2).to_broadcast([P, NT, E]), ALU.is_le))
            step(nc.vector.tensor_reduce(e_of[:], t_te[:], AX.X, ALU.add))
            step(nc.vector.tensor_tensor(t_tc[:], t_te[:], cum[:].unsqueeze(1).to_broadcast([P, NT, E]), ALU.mult))
            step(nc.vector.tensor_reduce(prev[:], t_tc[:], AX.X, ALU.max))
            step(nc.vector.tensor_tensor(within[:], iota_t[:], prev[:], ALU.subtract))
            step(nc.vector.tensor_scalar(within[:], within[:], float(P), None, ALU.mult))
            step(nc.vector.scalar_tensor_tensor(tile_row[:], e_of[:], float(STRIDE), within[:], ALU.mult, ALU.add))
            step(nc.vector.tensor_scalar(tile_expert[:, 1:NT + 1], e_of[:], float(E - 1), None, ALU.min))
            choices = choice[:].rearrange("p b k -> p (b k)")
            step(nc.vector.tensor_tensor(t_be[:], choices.unsqueeze(2).to_broadcast([LQ, 2 * B, E]),
                                         iota_e[0:LQ, :].unsqueeze(1).to_broadcast([LQ, 2 * B, E]), ALU.is_equal))
            step(nc.vector.tensor_tensor(t_bc[:], t_be[:], cum_ex[0:LQ, :].unsqueeze(1).to_broadcast([LQ, 2 * B, E]), ALU.mult))
            step(nc.vector.tensor_reduce(first_tile[:], t_bc[:], AX.X, ALU.add))
            step(nc.vector.scalar_tensor_tensor(row_of[:].rearrange("p b k -> p (b k)"), first_tile[:], float(P),
                                                rank[:].rearrange("p b k -> p (b k)"), ALU.mult, ALU.add))
            assert done[0] == N_PLAN

            def lo_of_rows(t, slot):
                dve.wait_ge(hT_hi, t + 1)
                nc.vector.tensor_tensor(hT_l[:, slot].rearrange("p k n -> p (k n)"), hT_ps[:, 0:2 * P],
                                        hT_h[:, slot].rearrange("p k n -> p (k n)").bitcast(F32),
                                        ALU.subtract).then_inc(hT_lo, 1)

            lo_of_rows(0, 0)

            def four_tiles(i):
                for k in range(4):
                    t = 4 * i + k
                    if there(t - 1, NT):
                        dve.wait_ge(hidT_made, t)
                        nc.vector.tensor_copy(hidT[:].rearrange("p j n -> p (j n)"), hidT_ps[:]).then_inc(hidT_done, 1)
                    if there(t + 1, NT):
                        lo_of_rows(t + 1, (k + 1) % 2)
                    if there(t, NT):
                        dve.wait_ge(silu_done, t + 1)
                        dve.wait_ge(up_made, t + 1)
                        nc.vector.tensor_tensor(hid[:], up_ps[k % 2][:], silu[:], ALU.mult).then_inc(hid_done, 1)

            over_tiles(four_tiles, dve)

            def last_four(i):
                for s in range(4):
                    b = 4 * i + s
                    dve.wait_ge(gx_in[s], 16 * (i + 1))
                    dve.wait_ge(g_in[s], 32 * (i + 1))
                    w = row_at(share, b)
                    nc.vector.scalar_tensor_tensor(g_sum[:, s, :], g_rows[:, s, 0, :], w[:, 0:1], g_x[:, s, :],
                                                   ALU.mult, ALU.add).then_inc(gsum_done, 1)
                    dve.wait_ge(gsum_done, b + 1)
                    if not known(i) or i > 0:
                        dve.wait_ge(out_store[s], 16 * i)
                    nc.vector.scalar_tensor_tensor(g_out[:, s, :], g_rows[:, s, 1, :], w[:, 1:2], g_sum[:, s, :],
                                                   ALU.mult, ALU.add).then_inc(gout_done, 1)

            last_four(0)
            with dve.Fori(1, B // 4) as i:
                last_four(i)

        @block.tensor
        def _(pe):
            mm = nc.tensor.matmul

            def split_product(dst, pairs):
                todo = [(w, m) for wh, wl, mh, ml in pairs for w, m in ((wh, mh), (wh, ml), (wl, mh))]
                for n, (w, m) in enumerate(todo):
                    last = mm(dst, w, m, start=n == 0, stop=n == len(todo) - 1)
                return last

            def make(a, k, pair):
                odd, step, kind, arg = a.items[k]
                dst = A_ps[a.bank(k)]
                if not a.first or k >= 2:
                    if k >= 2:
                        if a.items[k - 2][2] == "V":
                            pe.wait_ge(v_done, a.values(k - 2))
                        else:
                            pe.wait_ge(lo_done, a.split(k - 2))
                    else:
                        pe.wait_ge(lo_done, a.split0 - 1 + k)
                slot = 1 - odd
                if kind == "yT":
                    slot = 0 if step < 0 else odd
                    pe.wait_ge(y_in[slot], 32 * (1 if a.first else pair + 2))
                    for t in range(KT):
                        last = nc.tensor.transpose(dst[:, t * KR:t * KR + KR], y_sb[:, slot, t, arg * P:arg * P + P],
                                                   ident[0:KR, 0:KR])
                elif kind == "xT":
                    pe.wait_ge(xn_done, 2 * (0 if a.first else pair + 1) + arg + 1)
                    for t in range(2):
                        last = nc.tensor.transpose(dst[:, t * LQ:t * LQ + LQ], xn[:, arg, t * P:t * P + P],
                                                   ident[0:LQ, 0:LQ])
                elif kind == "K":
                    if arg == 0:
                        pe.wait_ge(lo_done, context_split(a, odd))
                    c = slice(arg * P, arg * P + P)
                    last = product_ctx(dst[:, 0:LKE], c, slot, slice(0, LKE), True)
                elif kind == "q":
                    if arg == 0:
                        pe.wait_ge(lo_done, a.split(a.find(1, "xT", 1)))
                        if a.first:
                            pe.wait_ge(w_lo, 3)
                    c = slice(arg * P, arg * P + P)
                    last = split_product(dst[:, 0:2 * LQ], [(WqH[:, t, c], WqL[:, t, c], xT_h[:, t, :], xT_l[:, t, :])
                                                            for t in range(2)])
                else:
                    half, t = arg
                    if half:
                        slot = odd
                    c = slice(HD + half * 512, HD + half * 512 + 512)
                    last = product_ctx(dst[0:KR, :], c, slot, slice(t * KR, t * KR + KR), False)
                last.then_inc(made, 1)

            def product_ctx(dst, c, slot, rows, weights_stay):
                todo = [(WkvH[:, c], yA_h[:, slot, rows]), (WkvH[:, c], yA_l[:, slot, rows]),
                        (WkvL[:, c], yA_h[:, slot, rows]), (WkvT[:, c], yB[:, slot, rows]),
                        (WkvU[:, c], yB[0:CT, slot, rows])]
                for n, (w, y) in enumerate(todo):
                    last = mm(dst, w if weights_stay else y, y if weights_stay else w,
                              start=n == 0, stop=n == len(todo) - 1)
                return last

            def context_split(a, odd):
                if a.first:
                    return 2
                if odd:
                    return a.split(a.find(0, "yT", 1))
                return a.split_in_pair_before(1, "yT", 1)

            pe.wait_ge(consts, N_CONSTS)
            a = Ahead(None)
            for k in range(len(a.items)):
                if k == 4:
                    pe.wait_ge(w_lo, 2)
                make(a, k, None)

            def scores(a, i, odd, s, g):
                j, r = s // 2, s % 2
                if r == 0:
                    if odd:
                        pe.wait_ge(lo_done, a.split(a.find(0, "K", j)))
                    else:
                        pe.wait_ge(lo_done, a.split_in_pair_before(1, "q", j))
                if not known(g) or g >= 2:
                    pe.wait_ge(exp_done, g - 1)
                rows = slice(r * DK, r * DK + DK)
                q = slice(odd * LQ, odd * LQ + LQ)
                split_product(S_ps[r][0:LQ, 0:LKE], [(q_h[rows, j, q], q_l[rows, j, q], K_h[rows, j, :],
                                                      K_l[rows, j, :])]).then_inc(scores_made, 1)

            def turn_prob(i, odd, s, g):
                k, nth = (s - 1) % 2, 8 * (2 * i + odd) + (s - 1) // 2
                pe.wait_ge(exp_done, g + 1)
                if not known(g) or g >= 2:
                    pe.wait_ge(probT_odd if k else probT_even, nth)
                for t in range(KT):
                    last = nc.tensor.transpose(PT_ps[k][0:KR, t * LQ:t * LQ + LQ],
                                               prob[:, k, t * KR:t * KR + KR], ident[0:LQ, 0:LQ])
                last.then_inc(probT_made, 1)

            def weigh(a, i, odd, s, g):
                k, nth, head = s % 2, 8 * (2 * i + odd) + (s - 2) // 2, (s - 2) % H
                if head % HB == 0:
                    if not known(g) or g >= HB:
                        pe.wait_ge(O_done, 2 * (2 * i + odd) + head // HB)
                    if head:
                        pe.wait_ge(v_done, a.values(a.find(odd, "V", (1, KT - 1))))
                    elif odd:
                        pe.wait_ge(v_done, a.values(a.find(0, "V", (0, KT - 1))))
                    else:
                        pe.wait_ge(v_done, a.values_in_pair_before(1, "V", (0, KT - 1)))
                pe.wait_ge(probT_odd if k else probT_even, nth + 1)
                for t in range(KT):
                    last = mm(O_ps[0:LQ, head % HB * DK:head % HB * DK + DK], probT[:, k, t * LQ:t * LQ + LQ],
                              V[:, t, head * DK:head * DK + DK], start=t == 0, stop=t == KT - 1)
                last.then_inc(pv_made, 1)

            def turn_O(half):
                for j in range(4):
                    last = nc.tensor.transpose(C_ps[:, j * LQ:j * LQ + LQ],
                                               O_sb[:, (4 * half + j) * P:(4 * half + j) * P + P], ident[0:LQ, 0:LQ])
                last.then_inc(OT_made, 1)

            def after_attention(b, s, odd):
                if s == 1 and there(b - 2, B):
                    pe.wait_ge(chosen_done, b - 1)
                    pe.wait_ge(gates_done, b - 1)
                    mm(C_ps[0:LQ, 0:E], before[:], chosen[:], start=True, stop=True)
                    mm(C_ps[:, E:2 * E], ones[:], chosen[:], start=True, stop=True).then_inc(counts_made, 1)
                if s == 3 and there(b - 1, B):
                    pe.wait_ge(O_done, 2 * b)
                    if not known(b) or b >= 2:
                        pe.wait_ge(running_done, b - 1)
                    turn_O(1)
                if s == 5 and there(b - 1, B):
                    pe.wait_ge(OT_lo, 2 * b)
                    if known(b) and b == 1:
                        pe.wait_ge(w_lo, 4)
                    split_product(C_ps[0:LQ, 0:C], [(OT_h[:, j, :], OT_l[:, j, :], WpH[:, j, :], WpL[:, j, :])
                                                    for j in range(NJ)]).then_inc(proj_made, 1)
                if s == 8 and there(b - 1, B):
                    pe.wait_ge(x2_done, b)
                    pe.wait_ge(hn_done, b)
                    for t in range(2):
                        last = nc.tensor.transpose(C_ps[:, t * LQ:t * LQ + LQ], hn[:, 1 - odd, t * P:t * P + P],
                                                   ident[0:LQ, 0:LQ])
                    last.then_inc(hnT_made, 1)
                if s == 11 and there(b, B):
                    pe.wait_ge(O_done, 2 * b + 1)
                    if not known(b) or b >= 1:
                        pe.wait_ge(hnT_done, b)
                    turn_O(0)
                if s == 13 and there(b - 1, B):
                    pe.wait_ge(hnT_done, b)
                    if there(b, B):
                        pe.wait_ge(OT_lo, 2 * b + 1)
                    if known(b) and b == 1:
                        pe.wait_ge(small_in, 32)
                    for t in range(2):
                        last = mm(C_ps[0:LQ, 0:E], hnT[:, t, :], gw[:, t, :], start=t == 0, stop=t == 1)
                    last.then_inc(logits_made, 1)

            def pair(i):
                a = Ahead(i) if there(i, NP) else None
                for odd in (0, 1):
                    b = 2 * i + odd
                    for s in range(H):
                        g = H * b + s
                        if there(g, B * H):
                            scores(a, i, odd, s, g)
                        items = a.at(odd, s) if a else []
                        for k in items[:1]:
                            make(a, k, i)
                        if there(g - 1, B * H):
                            turn_prob(i, odd, s, g - 1)
                        after_attention(b, s, odd)
                        if there(g - 2, B * H):
                            weigh(a, i, odd, s, g - 2)
                        for k in items[1:]:
                            make(a, k, i)

            over_pairs(pe, pair)

            pe.wait_ge(plan, N_PLAN)
            pe.wait_ge(running_done, B)

            def turn_rows(i, t, slot):
                pe.wait_ge(h_in_ld[slot], 16 * (i + 1))
                for j in range(2):
                    last = nc.tensor.transpose(hT_ps[:, j * P:j * P + P], h_in[:, slot, j * P:j * P + P], ident[:])
                last.then_inc(hT_made, 1)

            def experts_from(i, first, n):
                c = 4 * i + first + 1
                return nc.values_load_multi_w_load_instructions(
                    tile_expert[0:1, c:c + n] if known(i) else tile_expert[0:1, bass.ds(c, n)],
                    engines=(mybir.EngineType.PE,), min_val=0, max_val=E - 1)[1]

            def hidden(dst, e, slot, half):
                c = slice(half * FF, half * FF + FF)
                return split_product(dst, [(hT_h[:, slot, j, :], hT_l[:, slot, j, :], Wgu[:, e, 0, j, c], Wgu[:, e, 1, j, c])
                                           for j in range(2)])

            turn_rows(0, 0, 0)

            def four_tiles(i):
                experts = experts_from(i, -1, 4) + experts_from(i, 3, 1)
                for k in range(4):
                    t = 4 * i + k
                    if there(t, NT):
                        e = experts[k + 1]
                        pe.wait_ge(hT_lo, t + 1)
                        pe.wait_ge(wgu_lo, e + 1)
                        if not known(t) or t >= 2:
                            pe.wait_ge(silu_done, t - 1)
                        hidden(gate_ps[k % 2][:], e, k % 2, 0).then_inc(gate_made, 1)
                    if there(t - 1, NT):
                        pe.wait_ge(hid_done, t)
                        if not known(t) or t >= 2:
                            pe.wait_ge(hidT_done, t - 1)
                        for j in range(FJ):
                            last = nc.tensor.transpose(hidT_ps[:, j * P:j * P + P], hid[:, j * P:j * P + P], ident[:])
                        last.then_inc(hidT_made, 1)
                    if there(t + 1, NT):
                        turn_rows(i if k < 3 else i + 1, t + 1, (k + 1) % 4)
                    if there(t, NT):
                        if not known(t) or t >= 2:
                            pe.wait_ge(hid_done, t - 1)
                        hidden(up_ps[k % 2][:], e, k % 2, 1).then_inc(up_made, 1)
                    if there(t - 1, NT):
                        pe.wait_ge(hidT_done, t)
                        if known(t) and t == 1:
                            pe.wait_ge(wd_early, 16)
                            pe.wait_ge(wd_in, 16)
                        if not known(t) or t >= 3:
                            pe.wait_ge(y_done, t - 2)
                        for j in range(FJ):
                            last = mm(down_ps[(k + 1) % 2][:, 0:C], hidT[:, j, :], Wd[:, experts[k], j, :],
                                      start=j == 0, stop=j == FJ - 1)
                        last.then_inc(down_made, 1)

            over_tiles(four_tiles, pe)


_INS = ["x", "ctx_768", "L0_xattn_Wq", "L0_xattn_Wkv", "L0_xattn_Wproj", "L0_xattn_bproj",
        "L0_ffn_gate_w", "L0_ffn_gate_up_w", "L0_ffn_down_w"]


def kernel(**inputs):
    from concourse import bacc
    from concourse.bass_utils import run_bass_kernel_spmd

    nc = bacc.Bacc("TRN2", target_bir_lowering=False, num_devices=1)
    arrays, args = {}, []
    for name in _INS:
        a = np.ascontiguousarray(inputs[name])
        arrays[f"in_{name}"] = a
        args.append(nc.dram_tensor(f"in_{name}", a.shape, mybir.dt.from_np(a.dtype), kind="ExternalInput").ap())
    out = nc.dram_tensor("out", (B, LQ, C), F32, kind="ExternalOutput").ap()
    attention_and_experts(nc, *args, out)
    r = run_bass_kernel_spmd(nc, [arrays], core_ids=[0])
    return r.results[0]["out"]
```

```python
from contextlib import ExitStack

import numpy as np
import concourse.bass as bass
from concourse import mybir
from concourse.alu_op_type import AluOpType as ALU

F32 = mybir.dt.float32
F32R = mybir.dt.float32r
BF16 = mybir.dt.bfloat16
I32 = mybir.dt.int32
U32 = mybir.dt.uint32
ACT = mybir.ActivationFunctionType
AX = mybir.AxisListType

B, LQ, C = 32, 112, 256
LKV, CTX = 375, 192
H, DK = 16, 64
HD = H * DK
P = 128
NP = B // 2
KT, KR = 3, LKV // 3
LKE = LKV + 1
NJ = HD // P
HB = H // 2
CT = CTX - P
EPS = 1e-5
SCALE = DK ** -0.5

G = 4
E, FF = 8, 512
TOK = B * LQ
CAP = TOK // P * P
assert CAP == TOK
STRIDE = CAP + P
NT = (2 * TOK + E * (P - 1)) // P
assert NT % 4 == 3
IDLE = NT - 2 * TOK // P
FJ = FF // P
W = C + 2



def ahead(odd, step):
    out = []
    if step == 0 and odd:
        out += [("xT", 0), ("xT", 1)]
    if step % 2 == 1:
        out.append(("K", step // 2))
        if odd:
            out.append(("q", step // 2))
    if step in (2, 4, 6):
        out.append(("V", (1, step // 2 - 1)))
    if step in (10, 12, 14):
        out.append(("V", (0, step // 2 - 5)))
    if step == 8:
        out += [("yT", 0), ("yT", 1)]
    return [(odd, step, kind, a) for kind, a in out]


PAIR = [it for odd in (0, 1) for s in range(H) for it in ahead(odd, s)]
assert len(PAIR) % 2 == 0
START = [(1, -1, "yT", 0), (1, -1, "yT", 1)] + [
    it for s in range(H) for it in ahead(1, s) if not (it[2] == "V" and it[3][0] == 1)]
LAST = [it for it in PAIR if it[2] not in ("q", "xT", "yT") and not (it[0] and it[2] == "K")
        and not (it[0] and it[2] == "V" and it[3][0] == 0)]


def n_split(items):
    return sum(it[2] != "V" for it in items)


class Ahead:

    def __init__(self, i):
        self.items = START if i is None else LAST if isinstance(i, int) and i == NP - 1 else PAIR
        k = 0 if i is None else i
        base = 0 if i is None else 1
        self.first = i is None
        self.n0 = base * len(START) + k * len(PAIR)
        self.split0 = base * n_split(START) + k * n_split(PAIR)
        self.v0 = base * (len(START) - n_split(START)) + k * (len(PAIR) - n_split(PAIR))
        self.bank0 = base * len(START) % 2

    def at(self, odd, step):
        return [k for k, it in enumerate(self.items) if it[0] == odd and it[1] == step]

    def find(self, odd, kind, a):
        return [k for k, it in enumerate(self.items) if (it[0], it[2], it[3]) == (odd, kind, a)][0]

    def bank(self, k):
        return (self.bank0 + k) % 2

    def made(self, k):
        return self.n0 + k + 1

    def split(self, k):
        return self.split0 + n_split(self.items[:k + 1])

    def values(self, k):
        return self.v0 + k + 1 - n_split(self.items[:k + 1])

    def split_in_pair_before(self, odd, kind, a):
        k = [n for n, it in enumerate(PAIR) if (it[0], it[2], it[3]) == (odd, kind, a)][0]
        return self.split0 - n_split(PAIR[k + 1:])

    def values_in_pair_before(self, odd, kind, a):
        k = [n for n, it in enumerate(PAIR) if (it[0], it[2], it[3]) == (odd, kind, a)][0]
        return self.v0 - (len(PAIR[k + 1:]) - n_split(PAIR[k + 1:]))


def known(v):
    return isinstance(v, int)


def there(v, end):
    return not known(v) or 0 <= v < end


def over_pairs(eng, body, first=1, end=NP - 1, tail=True):
    for i in range(first):
        body(i)
    with eng.Fori(first, end) as i:
        body(i)
    for i in range(end, NP):
        body(i)
    if tail:
        body(NP)


def over_tiles(eng, body):
    body(0)
    with eng.Fori(1, NT // 4) as i:
        body(i)
    body(NT // 4)


def dram_at(t, b):
    return t[b] if known(b) else t[bass.ds(b, 1)].rearrange("o q c -> (o q) c")


def attention_and_experts(nc, x, ctx_in, Wq, Wkv, Wproj, bproj, gate_w, gate_up_w, down_w, out):
    x2_dram = nc.dram_tensor("x2_scratch", [B, LQ, C], F32).ap()
    bins = nc.dram_tensor("bins", [E * STRIDE + IDLE * P, W], F32).ap()
    y_dram = nc.dram_tensor("expert_rows", [2 * TOK + (E + IDLE) * P, C], F32).ap()

    with ExitStack() as stack:
        base = (nc.sbuf_base + 63) // 64 * 64
        size = (nc.sbuf_usable_end - base) // 64 * 64 - 64
        stack.enter_context(nc.sbuf_tensor("arena", [P, size // 4], F32))
        place = {"at": base + 64}

        def sb(name, shape, dt):
            bytes_ = int(np.prod(shape[1:])) * (2 if dt == BF16 else 4)
            t = nc.alloc_sbuf_tensor_at(name, shape, dt, offset=place["at"])
            place["at"] += (bytes_ + 31) // 32 * 32
            assert place["at"] <= base + size, name
            return t

        def sem(name):
            return stack.enter_context(nc.semaphore(name))

        ident = sb("ident", [P, P], F32)
        before = sb("before", [LQ, LQ], BF16)
        ones = sb("ones", [LQ, P], BF16)
        iota_e = sb("iota_e", [P, E], F32)
        le_mask = sb("le_mask", [P, E, E], F32)
        iota_tile = sb("iota_tile", [P, CAP // P], F32)
        iota_t = sb("iota_t", [P, NT], F32)
        iota_p = sb("iota_p", [P, E], F32)
        running = sb("running", [P, E], F32)
        tile_row = sb("tile_row", [P, NT], I32)
        tile_expert = sb("tile_expert", [P, NT + 5], I32)
        pad_row = sb("pad_row", [P, E], I32)
        dest = sb("dest", [LQ, 2], F32)
        dest_now = sb("dest_now", [P, 4], I32)
        share_now = sb("share_now", [P, 4], F32)
        wgu_at = place["at"]
        raw = sb("raw", [P, 2, 2 * 2 * FF], F32)
        shared_from = place["at"]

        WqH = sb("WqH", [P, 2, HD], F32R)
        WqL = sb("WqL", [P, 2, HD], F32R)
        WkvH = sb("WkvH", [P, 2 * HD], F32R)
        WkvL = sb("WkvL", [P, 2 * HD], F32R)
        WkvT = sb("WkvT", [P, 2 * HD], F32R)
        WkvU = sb("WkvU", [CT, 2 * HD], F32R)
        y_sb = sb("y_sb", [KR, 2, KT, 2 * P], F32)
        yA_h = sb("yA_h", [P, 2, LKE], F32R)
        yA_l = sb("yA_l", [P, 2, LKE], F32R)
        yB = sb("yB", [P, 2, LKE], F32R)
        K_h = sb("K_h", [P, NJ, LKE], F32R)
        K_l = sb("K_l", [P, NJ, LKE], F32R)
        q_h = sb("q_h", [P, NJ, 2 * LQ], F32R)
        q_l = sb("q_l", [P, NJ, 2 * LQ], F32R)
        V = sb("V", [KR, KT, HD], F32)
        prob = sb("prob", [LQ, 2, LKV], F32)
        probT = sb("probT", [KR, 2, KT * LQ], F32)
        x_sb = sb("x_sb", [LQ, 2, C], F32)
        assert place["at"] >= shared_from + (E - 1) * 2 * 2 * 2 * FF * 4
        WpH = sb("WpH", [P, NJ, C], F32R)
        WpL = sb("WpL", [P, NJ, C], F32R)
        gw = sb("gw", [P, 2, E], F32)
        bias = sb("bias", [LQ, C], F32)
        neg_max = sb("neg_max", [LQ, 2], F32)
        row_sum = sb("row_sum", [LQ, 2, HB], F32)
        inv_sum = sb("inv_sum", [LQ, HB], F32)
        O_sb = sb("O_sb", [LQ, HD], F32)
        OT_h = sb("OT_h", [P, NJ, LQ], F32R)
        OT_l = sb("OT_l", [P, NJ, LQ], F32R)
        xn = sb("xn", [LQ, 2, C], F32)
        xT_h = sb("xT_h", [P, 2, 2 * LQ], F32R)
        xT_l = sb("xT_l", [P, 2, 2 * LQ], F32R)
        stat1 = sb("stat1", [LQ, 2, 6], F32)
        mv1 = sb("mv1", [LQ, 2, 2], F32)
        std1 = sb("std1", [LQ, 2, 2], F32)
        x_res = sb("x_res", [LQ, 2, C], F32)
        x_bias = sb("x_bias", [LQ, 2, C], F32)
        x2 = sb("x2", [LQ, 2, C], F32)
        hn = sb("hn", [LQ, 2, 2, W], F32)
        pad_rows = sb("pad_rows", [P, E, W], F32)
        stat2 = sb("stat2", [LQ, 6], F32)
        mv2 = sb("mv2", [LQ, 2], F32)
        std2 = sb("std2", [LQ, 2], F32)
        minus_half = sb("minus_half", [LQ, 2], F32)
        hnT = sb("hnT", [P, 2, LQ], F32)
        neg_top = sb("neg_top", [LQ, 1], F32)
        gates = sb("gates", [LQ, E], F32)
        top = sb("top", [LQ, E], F32)
        top_i = sb("top_i", [LQ, E], U32)
        top_f = sb("top_f", [LQ, 2], F32)
        onehot = sb("onehot", [LQ, 2, E], F32)
        chosen = sb("chosen", [LQ, E], BF16)
        bin_at = sb("bin_at", [LQ, E], F32)
        picked = sb("picked", [LQ, 2, E], F32)
        rank2 = sb("rank2", [LQ, 2], F32)
        bin_row = sb("bin_row", [LQ, 2, 2], I32)
        top_sum = sb("top_sum", [LQ, 1], F32)
        inv_top = sb("inv_top", [LQ, 1], F32)

        part1_end = place["at"]
        wd_at = base + size - E * FJ * C * 4
        early = -(-(part1_end - wd_at) // (FJ * C * 4))
        place["at"] = wgu_at
        Wgu = sb("Wgu", [P, E, 2, 2, 2 * FF], F32R)
        scratch_at = place["at"]
        h_in = sb("h_in", [P, 4, W], F32)
        hT_h = sb("hT_h", [P, 2, 2, P], F32R)
        hT_l = sb("hT_l", [P, 2, 2, P], F32R)
        silu = sb("silu", [P, FF], F32)
        hid = sb("hid", [P, FF], F32)
        hidT = sb("hidT", [P, FJ, P], F32)
        y_out = sb("y_out", [P, 2, C], F32)
        x2_early = min((wd_at - place["at"]) // (G * C * 4), B // G)
        g_x = [sb(f"g_x{n}", [LQ, G, C], F32) for n in range(x2_early)]
        assert place["at"] <= wd_at
        place["at"] = wd_at
        Wd = sb("Wd", [P, E, FJ, C], F32)
        place["at"] = scratch_at
        t_cmp = sb("t_cmp", [P, E, CAP // P], F32)
        n_tiles = sb("n_tiles", [P, E], F32)
        t_ee = sb("t_ee", [P, E, E], F32)
        cum = sb("cum", [P, E], F32)
        cum_ex = sb("cum_ex", [P, E], F32)
        t_te = sb("t_te", [P, NT, E], F32)
        t_tc = sb("t_tc", [P, NT, E], F32)
        e_of = sb("e_of", [P, NT], F32)
        prev = sb("prev", [P, NT], F32)
        within = sb("within", [P, NT], F32)
        place["at"] = shared_from
        g_rows = sb("g_rows", [LQ, B // G, 2, G, C], F32)
        g_x += [sb(f"g_x{n}", [LQ, G, C], F32) for n in range(x2_early, B // G)]

        banks = [stack.enter_context(nc.psum_tensor(f"bank{k}", [P, 512], F32)) for k in range(8)]
        S_ps, PT_ps, A_ps, O_ps, C_ps = banks[0:2], banks[2:4], banks[4:6], banks[6], banks[7]
        gate_ps, up_ps, hT_ps, hidT_ps = banks[0:2], banks[2:4], banks[4], banks[5]
        down_ps = banks[6:8]

        raw_in = [sem(f"raw_in{k}") for k in range(2)]
        small_in = sem("small_in")
        consts = sem("consts")
        passed = sem("passed")
        w_hi, w_lo = sem("w_hi"), sem("w_lo")
        wp_done = sem("wp_done")
        y_in = [sem(f"y_in{k}") for k in range(2)]
        x_in = sem("x_in")
        xres_in = [sem(f"xres_in{k}") for k in range(2)]
        made = sem("made")
        hi_done, lo_done = sem("hi_done"), sem("lo_done")
        v_done = sem("v_done")
        scores_made, max_done, exp_done = sem("scores_made"), sem("max_done"), sem("exp_done")
        probT_made = sem("probT_made")
        probT_even, probT_odd = sem("probT_even"), sem("probT_odd")
        pv_made = sem("pv_made")
        inv_done, O_done = sem("inv_done"), sem("O_done")
        OT_made, OT_hi, OT_lo = sem("OT_made"), sem("OT_hi"), sem("OT_lo")
        proj_made, x2_done, x2_out = sem("proj_made"), sem("x2_done"), [sem("x2_out0"), sem("x2_out1")]
        st1, ag1, eps1, rs1, xn_done = sem("st1"), sem("ag1"), sem("eps1"), sem("rs1"), sem("xn_done")
        xb_done = sem("xb_done")
        st2, ag2, eps2, rs2, hn_done = sem("st2"), sem("ag2"), sem("eps2"), sem("rs2"), sem("hn_done")
        hnT_made, hnT_done = sem("hnT_made"), sem("hnT_done")
        logits_made, top_neg, gates_done = sem("logits_made"), sem("top_neg"), sem("gates_done")
        top_done, topi_done, topf_done = sem("top_done"), sem("topi_done"), sem("topf_done")
        onehot_done, chosen_done = sem("onehot_done"), sem("chosen_done")
        counts_made, binat_done, running_done = sem("counts_made"), sem("binat_done"), sem("running_done")
        picked_done, rank_done, row_done = sem("picked_done"), sem("rank_done"), sem("row_done")
        tsum_done, tinv_done = sem("tsum_done"), sem("tinv_done")
        hn_twin = sem("hn_twin")
        kept, next_dest = sem("kept"), sem("next_dest")
        scattered = [sem("scattered0"), sem("scattered1")]
        pads_ready = sem("pads_ready")
        idle_out, pads_out, pads_late = sem("idle_out"), sem("pads_out"), sem("pads_late")
        plan = sem("plan")
        wd_early, wd_in = sem("wd_early"), sem("wd_in")
        wgu_raw = [sem(f"wgu_raw{e}") for e in range(E)]
        wgu_hi, wgu_hi0 = sem("wgu_hi"), sem("wgu_hi0")
        wgu_lo = [sem("wgu_lo_pool"), sem("wgu_lo_dve")]
        dest_done = sem("dest_done")
        h_in_ld = [sem(f"h_in{k}") for k in range(4)]
        hT_made, hT_hi, hT_lo = sem("hT_made"), sem("hT_hi"), sem("hT_lo")
        gate_made, up_made, silu_done, hid_done = sem("gate_made"), sem("up_made"), sem("silu_done"), sem("hid_done")
        hidT_made, hidT_done, down_made, y_done = sem("hidT_made"), sem("hidT_done"), sem("down_made"), sem("y_done")
        y_store = [sem("y_store0"), sem("y_store1")]
        gx_in = [sem("gx_early"), sem("gx_late")]
        g_in = [sem(f"g_in{n}") for n in range(B // G)]
        gsum_done, gout_done = sem("gsum_done"), sem("gout_done")
        out_store = sem("out_store")

        N_CONSTS = 19
        N_PLAN = 14
        block = stack.enter_context(nc.Block())

        def load_expert(eng, e):
            eng.dma_start(Wgu[:, e, 1].bitcast(F32), gate_up_w[e].rearrange("(k p) n -> p k n", p=P)).then_inc(wgu_raw[e], 16)

        @block.sync
        def _(sp):
            assert shared_from == wgu_at + 4 * 2 * 2 * 2 * FF

            def load_y(b, slot):
                rows = ctx_in[b:b + 1] if known(b) else ctx_in[bass.ds(b, 1)]
                rows = rows.rearrange("o (k p) c -> p (o k) c", p=KR)
                sp.dma_start(y_sb[:, slot, :, 0:CTX], rows).then_inc(y_in[slot], 16)
                sp.dma_start(y_sb[:, slot, :, CTX:2 * P], rows[:, :, P:CTX]).then_inc(y_in[slot], 16)

            def load_x(pair):
                rows = x[bass.ds(2 * pair, 2)] if not known(pair) else x[2 * pair:2 * pair + 2]
                sp.dma_start(x_sb[:], rows.rearrange("b q c -> q b c")).then_inc(x_in, 16)

            sp.sem_inc(x2_out[1], 16)
            load_y(0, 0)
            sp.dma_start(raw[:, 0, :], Wkv[0:P, :]).then_inc(raw_in[0], 16)
            load_x(0)
            sp.dma_start(raw[0:CT, 1, :], Wkv[P:CTX, :]).then_inc(raw_in[1], 16)
            sp.dma_start(raw[CT:P, 1, :], Wkv[P:CTX, :]).then_inc(raw_in[1], 16)
            load_y(1, 1)
            sp.dma_start(gw[:], gate_w.rearrange("(k p) e -> p k e", p=P)).then_inc(small_in, 16)
            sp.dma_start(bias[:], bproj.rearrange("(o c) -> o c", o=1).to_broadcast([LQ, C])).then_inc(small_in, 16)
            sp.wait_ge(w_lo, 1)
            sp.dma_start(raw[:, 0, :], Wq.rearrange("(k p) n -> p k n", p=P)).then_inc(raw_in[0], 16)
            sp.wait_ge(w_lo, 2)
            sp.dma_start(raw[:, 1, :], Wproj.rearrange("(k p) n -> p k n", p=P)).then_inc(raw_in[1], 16)
            a = Ahead(None)
            sp.wait_ge(made, a.made(1))
            load_y(2, 0)
            sp.wait_ge(xn_done, 2)
            load_x(1)
            sp.wait_ge(made, a.made([k for k, it in enumerate(START) if it[2:] == ("yT", 1)][1]))
            load_y(3, 1)
            sp.wait_ge(pads_ready, 1)
            for k in range(IDLE):
                r = E * STRIDE + k * P
                sp.dma_start(bins[r:r + P, :], pad_rows[:, k, :]).then_inc(idle_out, 16)

            def pair(i):
                a = Ahead(i)
                if known(i) and i == NP - 2:
                    sp.wait_ge(w_lo, 3)
                    sp.wait_ge(wp_done, 2)
                    load_expert(sp, 0)
                    sp.dma_start(Wd[:, early:E].rearrange("p e k n -> p (e k) n"),
                                 down_w[early:E].rearrange("e (k p) n -> p (e k) n", p=P)).then_inc(wd_early, 16)
                if known(i) and i == NP - 1:
                    sp.wait_ge(made, a.n0)
                    load_expert(sp, 1)
                for odd in (0, 1):
                    b = 2 * i + odd
                    if there(b, B):
                        if not known(b) or b >= 2:
                            sp.wait_ge(xb_done, b - 1)
                        sp.dma_start(x_res[:, odd, :], dram_at(x, b)).then_inc(xres_in[odd], 16)
                    if there(b - 1, B):
                        sp.wait_ge(x2_done, b)
                        sp.dma_start(dram_at(x2_dram, b - 1), x2[:, 1 - odd, :]).then_inc(x2_out[1 - odd], 16)
                    if not known(i) or i + 2 < NP:
                        sp.wait_ge(made, a.made(a.find(odd, "yT", 1)))
                        load_y(b + 4, odd)
                    if odd and (not known(i) or i + 2 < NP):
                        sp.wait_ge(xn_done, 2 * (i + 2))
                        load_x(i + 2)
                    if known(i) and i == NP - 1 and odd:
                        sp.wait_ge(made, a.n0 + len(a.items))
                        for e in (2, 3):
                            load_expert(sp, e)

            over_pairs(sp, pair, 1, NP - 2)

            sp.wait_ge(plan, 1)
            sp.wait_ge(pads_ready, 2)
            pad_starts = nc.values_load_multi_w_load_instructions(
                pad_row[0:1, E // 2:E], engines=(mybir.EngineType.SP,), min_val=0, max_val=E * STRIDE - P)[1]
            for e, start in zip(range(E // 2, E), pad_starts):
                sp.dma_start(bins[bass.ds(start, P), :], pad_rows[:, e, :]).then_inc(pads_late, 16)

            sp.wait_ge(plan, N_PLAN)
            sp.wait_ge(counts_made, B)
            sp.wait_ge(gates_done, B)
            sp.wait_ge(x2_out[0], 16 * NP)
            sp.wait_ge(x2_out[1], 16 * NP + 16)
            sp.wait_ge(scattered[0], 32 * NP)
            sp.wait_ge(scattered[1], 32 * NP)
            sp.wait_ge(pads_out, 16 * (E // 2))
            sp.wait_ge(pads_late, 16 * (E // 2))
            sp.wait_ge(idle_out, 16 * IDLE)

            def load_rows(t, slot):
                r = sp.value_load(tile_row[0:1, t:t + 1] if known(t) else tile_row[0:1, bass.ds(t, 1)],
                                  min_val=0, max_val=E * STRIDE + (IDLE - 1) * P)
                sp.dma_start(h_in[:, slot, :], bins[bass.ds(r, P), :]).then_inc(h_in_ld[slot], 16)

            def of(t, step):
                return t[step * G * LQ:step * G * LQ + G * LQ, :].rearrange("(b q) c -> q b c", q=LQ)

            for t in range(3):
                load_rows(t, t)
            x2_rows = x2_dram.rearrange("b q c -> (b q) c")

            def four_tiles(i):
                for k in range(4):
                    t = 4 * i + k
                    if there(t + 3, NT):
                        if not known(t) or t >= 1:
                            sp.wait_ge(hT_made, t)
                            sp.wait_ge(dest_done, t)
                        load_rows(t + 3, (k + 3) % 4)
                    if known(t) and 4 * (NT // 4) <= t < NT:
                        for n in range((t % 4) * 3, min((t % 4) * 3 + 3, x2_early)):
                            sp.dma_start(g_x[n][:], of(x2_rows, n)).then_inc(gx_in[0], 16)

            over_tiles(sp, four_tiles)

            for k in range(2):
                sp.wait_ge(y_store[k], 16 * ((NT + 1 - k) // 2))
            for n in range(B // G):
                for k in range(2):
                    sp.dma_start(g_rows[:, n, k], of(y_dram[k * TOK:k * TOK + TOK, :], n)).then_inc(g_in[n], 16)
                if n == 0:
                    for m in range(x2_early, B // G):
                        sp.dma_start(g_x[m][:], of(x2_rows, m)).then_inc(gx_in[1], 16)
            sp.wait_ge(out_store, 16 * (B // G))

        @block.gpsimd
        def _(pool):
            pool.memset(pad_rows[:], 0.0).then_inc(consts, 1)
            pool.iota(dest[:], [[TOK, 2]], base=0, channel_multiplier=1,
                      allow_small_or_imprecise_dtypes=True).then_inc(consts, 1)
            pool.memset(ident[:], 0.0).then_inc(consts, 1)
            pool.memset(before[:], 1.0).then_inc(consts, 1)
            pool.memset(ones[:], 1.0).then_inc(consts, 1)
            pool.memset(le_mask[:], 1.0).then_inc(consts, 1)
            pool.memset(minus_half[:], -0.5).then_inc(consts, 1)
            pool.memset(running[:], 0.0).then_inc(consts, 1)
            pool.memset(tile_expert[:], 0).then_inc(consts, 1)
            for t in (yA_h, yA_l, yB):
                pool.memset(t[:, :, LKV:LKE].bitcast(F32), 0.0).then_inc(consts, 1)
            pool.iota(iota_e[:], [[1, E]], base=0, channel_multiplier=0,
                      allow_small_or_imprecise_dtypes=True).then_inc(consts, 1)
            pool.iota(iota_tile[:], [[P, CAP // P]], base=0, channel_multiplier=0,
                      allow_small_or_imprecise_dtypes=True).then_inc(consts, 1)
            pool.iota(iota_t[:], [[1, NT]], base=0, channel_multiplier=0,
                      allow_small_or_imprecise_dtypes=True).then_inc(consts, 1)
            pool.iota(iota_p[:], [[STRIDE, E]], base=0, channel_multiplier=1,
                      allow_small_or_imprecise_dtypes=True).then_inc(consts, 1)
            pool.wait_ge(consts, N_CONSTS - 3)
            pool.affine_select(out=ident[:], in_=ident[:], compare_op=ALU.not_equal, fill=1.0, base=0,
                               pattern=[[-1, P]], channel_multiplier=1).then_inc(consts, 1)
            pool.iota(pad_rows[:, 0:IDLE, C:C + 1], [[P, IDLE], [1, 1]], base=2 * TOK + E * P, channel_multiplier=1,
                      allow_small_or_imprecise_dtypes=True).then_inc(pads_ready, 1)
            pool.affine_select(out=before[:], in_=before[:], compare_op=ALU.is_gt, fill=0.0, base=0,
                               pattern=[[1, LQ]], channel_multiplier=-1).then_inc(consts, 1)
            pool.affine_select(out=le_mask[:], in_=le_mask[:], compare_op=ALU.is_ge, fill=0.0, base=0,
                               pattern=[[1, E], [-1, E]], channel_multiplier=0).then_inc(consts, 1)

            def norm_x(pair):
                pool.wait_ge(ag1, 2 * pair + 2)
                pool.sem_inc(passed, 1)
                pool.tensor_scalar(std1[:, :, 0], mv1[:, :, 1], EPS, None, ALU.add).then_inc(eps1, 1)
                pool.wait_ge(eps1, pair + 1)
                pool.tensor_tensor(std1[:, :, 1], std1[:, :, 0], minus_half[:, 0:2], ALU.pow).then_inc(rs1, 1)
                if not known(pair) or pair > 0:
                    a = Ahead(pair - 2 if not known(pair) or pair > 1 else None)
                    pool.wait_ge(made, a.made(a.find(1, "xT", 1)))
                pool.wait_ge(rs1, pair + 1)
                pool.sem_inc(passed, 1)
                for r in range(2):
                    pool.tensor_scalar(xn[:, r, :], x_sb[:, r, :], mv1[:, r, 0:1], std1[:, r, 1:2],
                                       ALU.subtract, ALU.mult).then_inc(xn_done, 1)

            norm_x(0)

            wp_hi, wp_lo = (t[:].rearrange("p k n -> p (k n)") for t in (WpH, WpL))
            pool.wait_ge(raw_in[1], 48)
            pool.tensor_copy(wp_hi, raw[:, 1, :]).then_inc(wp_done, 1)
            pool.wait_ge(wp_done, 1)
            pool.tensor_tensor(wp_lo, raw[:, 1, :], wp_hi.bitcast(F32), ALU.subtract).then_inc(wp_done, 1)

            def scatter(b, slot):
                pool.wait_ge(row_done, b + 1)
                pool.wait_ge(hn_twin, b + 1)
                pool.wait_ge(kept, 2 * b + 2)
                pool.sem_inc(passed, 1)
                for k in range(2):
                    pool.indirect_dma_start(bins, bass.IndirectOffsetOnAxis(ap=bin_row[:, slot, k:k + 1], axis=0),
                                            hn[:, slot, k, :], None).then_inc(scattered[slot], 16)

            def lo_of_expert(e):
                pool.tensor_tensor(Wgu[:, e, 1], Wgu[:, e, 1].bitcast(F32), Wgu[:, e, 0].bitcast(F32),
                                   ALU.subtract).then_inc(wgu_lo[0], 1)

            def split_expert(e):
                pool.wait_ge(wgu_raw[e], 16)
                pool.tensor_copy(Wgu[:, e, 0], Wgu[:, e, 1].bitcast(F32)).then_inc(wgu_hi0, 1)
                pool.wait_ge(wgu_hi0, e + 1)
                lo_of_expert(e)

            def pair(i):
                for odd in (0, 1):
                    b = 2 * i + odd
                    if there(b, B):
                        pool.wait_ge(xres_in[odd], 16 * (i + 1))
                        if known(b) and b == 0:
                            pool.wait_ge(small_in, 32)
                        if not known(b) or b >= 2:
                            pool.wait_ge(x2_done, b - 1)
                        pool.tensor_tensor(x_bias[:, odd, :], x_res[:, odd, :], bias[:], ALU.add).then_inc(xb_done, 1)
                    if there(b - 2, B):
                        scatter(b - 2, odd)
                    if there(b - 1, B):
                        pool.wait_ge(ag2, b)
                        pool.sem_inc(passed, 1)
                        pool.tensor_scalar(std2[:, 0:1], mv2[:, 1:2], EPS, None, ALU.add).then_inc(eps2, 1)
                        pool.wait_ge(eps2, b)
                        pool.tensor_tensor(std2[:, 1:2], std2[:, 0:1], minus_half[:, 0:1], ALU.pow).then_inc(rs2, 1)
                        if not known(b) or b >= 3:
                            pool.wait_ge(scattered[1 - odd], 32 * (i - 1 + odd))
                        pool.wait_ge(rs2, b)
                        pool.sem_inc(passed, 1)
                        for k, signal in enumerate((hn_done, hn_twin)):
                            pool.tensor_scalar(hn[:, 1 - odd, k, 0:C], x2[:, 1 - odd, :], mv2[:, 0:1], std2[:, 1:2],
                                               ALU.subtract, ALU.mult).then_inc(signal, 1)
                    if known(i) and i == NP and not odd:
                        pool.wait_ge(wgu_hi, 4)
                        lo_of_expert(5)
                    if not odd and (not known(i) or i + 1 < NP):
                        norm_x(i + 1)
                    if known(i) and i == NP - 1 and not odd:
                        split_expert(0)
                        pool.wait_ge(idle_out, 16 * IDLE)
                        pool.iota(pad_rows[:, :, C:C + 1], [[P, E], [1, 1]], base=2 * TOK, channel_multiplier=1,
                                  allow_small_or_imprecise_dtypes=True).then_inc(pads_ready, 1)
                    if known(i) and i == NP - 1 and odd:
                        split_expert(1)

            over_pairs(pool, pair, 2)

            pool.wait_ge(plan, 1)
            pool.wait_ge(pads_ready, 2)
            for e in range(E // 2):
                pool.indirect_dma_start(bins, bass.IndirectOffsetOnAxis(ap=pad_row[:, e:e + 1], axis=0),
                                        pad_rows[:, e, :], None).then_inc(pads_out, 16)

            def four_tiles(i):
                for k in range(4):
                    t = 4 * i + k
                    if there(t - 1, NT):
                        pool.wait_ge(y_done, t)
                        pool.wait_ge(dest_done, t)
                        pool.sem_inc(passed, 1)
                        pool.indirect_dma_start(
                            y_dram, bass.IndirectOffsetOnAxis(ap=dest_now[:, (k + 3) % 4:(k + 3) % 4 + 1], axis=0),
                            y_out[:, (k + 1) % 2, :], None).then_inc(y_store[(k + 1) % 2], 16)

            over_tiles(pool, four_tiles)

        @block.scalar
        def _(act):
            def hi_of_weight(dst, slot, loads, scale=1.0):
                act.wait_ge(raw_in[slot], 16 * loads)
                nc.scalar.mul(dst, raw[:, slot, :], scale).then_inc(w_hi, 1)

            def evacuate(a, k):
                odd, step, kind, arg = a.items[k]
                src = A_ps[a.bank(k)]
                act.wait_ge(made, a.made(k))
                if kind == "V":
                    half, t = arg
                    nc.scalar.copy(V[:, t, half * 512:half * 512 + 512], src[0:KR, :]).then_inc(v_done, 1)
                elif kind == "K":
                    nc.scalar.copy(K_h[:, arg, :], src[:, 0:LKE]).then_inc(hi_done, 1)
                elif kind == "q":
                    nc.scalar.copy(q_h[:, arg, :], src[:, 0:2 * LQ]).then_inc(hi_done, 1)
                elif kind == "yT":
                    slot = 0 if step < 0 else odd
                    dst = (yA_h if arg == 0 else yB)[:, slot, 0:LKV]
                    nc.scalar.copy(dst, src[:, 0:LKV]).then_inc(hi_done, 1)
                else:
                    nc.scalar.copy(xT_h[:, :, arg * LQ:arg * LQ + LQ],
                                   src[:, 0:2 * LQ].rearrange("p (k q) -> p k q", k=2)).then_inc(hi_done, 1)

            def hi_of_experts(first, end):
                for e in range(first, end):
                    act.wait_ge(wgu_raw[e], 16)
                    nc.scalar.copy(Wgu[:, e, 0], Wgu[:, e, 1].bitcast(F32)).then_inc(wgu_hi, 1)

            a = Ahead(None)
            evacuate(a, 0)
            evacuate(a, 1)
            hi_of_weight(WkvH[:], 0, 1)
            hi_of_weight(WkvT[:], 1, 2)
            evacuate(a, 2)
            evacuate(a, 3)
            hi_of_weight(WqH[:].rearrange("p k n -> p (k n)"), 0, 2, SCALE)
            for k in range(4, len(a.items)):
                evacuate(a, k)

            def pair(i):
                a = Ahead(i) if there(i, NP) else None
                for odd in (0, 1):
                    b = 2 * i + odd
                    for s in range(H):
                        g = H * b + s
                        items = a.at(odd, s) if a else []
                        short = items[:1] if s in (0, 8) else []
                        for k in short:
                            evacuate(a, k)
                        if there(g, B * H):
                            act.wait_ge(max_done, g + 1)
                            if not known(g) or g >= 2:
                                act.wait_ge(probT_made, g - 1)
                            nc.scalar.activation(prob[:, s % 2, :], S_ps[s % 2][0:LQ, 0:LKV], ACT.Exp,
                                                 bias=neg_max[:, s % 2:s % 2 + 1],
                                                 accum_out=row_sum[:, s // HB, s % HB:s % HB + 1]).then_inc(exp_done, 1)
                        for k in items[len(short):1]:
                            evacuate(a, k)
                        if s % 2 == 1 and there(g - 1, B * H):
                            act.wait_ge(probT_made, g)
                            if not known(g) or g >= 3:
                                act.wait_ge(pv_made, g - 2)
                            nc.scalar.copy(probT[:, 0, :], PT_ps[0][0:KR, 0:KT * LQ]).then_inc(probT_even, 1)
                        if known(i) and i == NP and not odd and s == 1:
                            act.wait_ge(pv_made, B * H)
                            for e in range(4, E):
                                load_expert(act, e)
                        if s in (3, 11) and there(b - (s == 3), B):
                            half = s == 3
                            n = 2 * (b - half) + half
                            act.wait_ge(OT_made, n + 1)
                            nc.scalar.copy(OT_h[:, 4 * half:4 * half + 4, :].rearrange("p j q -> p (j q)"),
                                           C_ps[:, 0:4 * LQ]).then_inc(OT_hi, 1)
                        for k in items[1:]:
                            evacuate(a, k)
                        if s == 13 and there(b - 1, B):
                            act.wait_ge(top_neg, b)
                            nc.scalar.activation(gates[:], C_ps[0:LQ, 0:E], ACT.Exp,
                                                 bias=neg_top[:, 0:1]).then_inc(gates_done, 1)
                        if known(i) and i == NP and not odd and s in (3, 13):
                            hi_of_experts(*((2, 7) if s == 3 else (7, E)))

            over_pairs(act, pair)

            act.wait_ge(plan, N_PLAN)
            act.wait_ge(counts_made, B)
            act.wait_ge(x2_out[0], 16 * NP)
            act.wait_ge(x2_out[1], 16 * NP + 16)
            act.wait_ge(scattered[0], 32 * NP)
            act.wait_ge(scattered[1], 32 * NP)

            def hi_of_rows(t, slot):
                act.wait_ge(hT_made, t + 1)
                nc.scalar.copy(hT_h[:, slot].rearrange("p k n -> p (k n)"), hT_ps[:, 0:2 * P]).then_inc(hT_hi, 1)

            hi_of_rows(0, 0)
            act.dma_start(Wd[:, 0:early].rearrange("p e k n -> p (e k) n"),
                          down_w[0:early].rearrange("e (k p) n -> p (e k) n", p=P)).then_inc(wd_in, 16)

            def four_tiles(i):
                for k in range(4):
                    t = 4 * i + k
                    if there(t, NT):
                        act.wait_ge(gate_made, t + 1)
                        if not known(t) or t >= 1:
                            act.wait_ge(hid_done, t)
                        nc.scalar.activation(silu[:], gate_ps[k % 2][:], ACT.Silu).then_inc(silu_done, 1)
                    if there(t + 1, NT):
                        hi_of_rows(t + 1, (k + 1) % 2)
                    if there(t - 1, NT):
                        act.wait_ge(down_made, t)
                        if not known(t) or t >= 3:
                            act.wait_ge(y_store[(k + 1) % 2], 16 * (2 * i + (k - 1) // 2))
                        act.wait_ge(dest_done, t)
                        nc.scalar.mul(y_out[:, (k + 1) % 2, :], down_ps[(k + 1) % 2][:, 0:C],
                                      share_now[:, (k + 3) % 4:(k + 3) % 4 + 1]).then_inc(y_done, 1)

            over_tiles(act, four_tiles)

            for n in range(B // G):
                act.wait_ge(gout_done, n + 1)
                act.dma_start(out[n * G:n * G + G].rearrange("b q c -> q b c"), g_rows[:, n, 0]).then_inc(out_store, 16)

        @block.vector
        def _(dve):
            def norm_x(pair):
                dve.wait_ge(x_in, 16 * (pair + 1))
                if not known(pair) or pair > 0:
                    dve.wait_ge(xn_done, 2 * pair)
                for r in range(2):
                    nc.vector.bn_stats(stat1[:, r, :], x_sb[:, r, :]).then_inc(st1, 1)
                for r in range(2):
                    dve.wait_ge(st1, 2 * pair + 1 + r)
                    dve.sem_inc(passed, 1)
                    nc.vector.bn_aggr(mv1[:, r, :], stat1[:, r, :]).then_inc(ag1, 1)

            def low_part(a, k):
                odd, step, kind, arg = a.items[k]
                if kind == "V":
                    return
                src = A_ps[a.bank(k)]
                dve.wait_ge(hi_done, a.split(k))
                if kind == "K":
                    lo, ps, hi = K_l[:, arg, :], src[:, 0:LKE], K_h[:, arg, :]
                elif kind == "q":
                    lo, ps, hi = q_l[:, arg, :], src[:, 0:2 * LQ], q_h[:, arg, :]
                elif kind == "yT":
                    slot = 0 if step < 0 else odd
                    if arg == 0:
                        lo, ps, hi = yA_l[:, slot, 0:LKV], src[:, 0:LKV], yA_h[:, slot, 0:LKV]
                    else:
                        lo, ps, hi = yB[CT:P, slot, 0:LKV], src[CT:P, 0:LKV], yB[CT:P, slot, 0:LKV]
                else:
                    lo, hi = xT_l[:, :, arg * LQ:arg * LQ + LQ], xT_h[:, :, arg * LQ:arg * LQ + LQ]
                    ps = src[:, 0:2 * LQ].rearrange("p (k q) -> p k q", k=2)
                nc.vector.tensor_tensor(lo, ps, hi.bitcast(F32), ALU.subtract).then_inc(lo_done, 1)

            a = Ahead(None)
            low_part(a, 0)
            low_part(a, 1)
            norm_x(0)
            dve.wait_ge(w_hi, 1)
            nc.vector.tensor_tensor(WkvL[:], raw[:, 0, :], WkvH[:].bitcast(F32), ALU.subtract).then_inc(w_lo, 1)
            dve.wait_ge(w_hi, 2)
            nc.vector.tensor_tensor(WkvU[:], raw[0:CT, 1, :], WkvT[0:CT, :].bitcast(F32), ALU.subtract).then_inc(w_lo, 1)
            low_part(a, 2)
            low_part(a, 3)
            dve.wait_ge(w_hi, 3)
            nc.vector.scalar_tensor_tensor(WqL[:].rearrange("p k n -> p (k n)"), raw[:, 0, :], SCALE,
                                           WqH[:].rearrange("p k n -> p (k n)").bitcast(F32),
                                           ALU.mult, ALU.subtract).then_inc(w_lo, 1)
            for k in range(4, len(a.items)):
                low_part(a, k)

            def invert_sums(n, k):
                dve.wait_ge(exp_done, HB * n + HB)
                nc.vector.reciprocal(inv_sum[:], row_sum[:, k, :]).then_inc(inv_done, 1)

            def normalise(n, k):
                dve.wait_ge(inv_done, n + 1)
                dve.wait_ge(pv_made, HB * n + HB)
                nc.vector.tensor_tensor(O_sb[:, k * 512:k * 512 + 512].rearrange("p (h d) -> p h d", h=HB),
                                        O_ps[0:LQ, :].rearrange("p (h d) -> p h d", h=HB),
                                        inv_sum[:].unsqueeze(2).to_broadcast([LQ, HB, DK]),
                                        ALU.mult).then_inc(O_done, 1)

            def residual(i, b, slot):
                dve.wait_ge(proj_made, b + 1)
                dve.wait_ge(xb_done, b + 1)
                if not known(b) or b >= 2:
                    dve.wait_ge(x2_out[slot], 16 * i)
                nc.vector.tensor_tensor(x2[:, slot, :], C_ps[0:LQ, 0:C], x_bias[:, slot, :], ALU.add).then_inc(x2_done, 1)
                dve.wait_ge(x2_done, b + 1)
                nc.vector.bn_stats(stat2[:], x2[:, slot, :]).then_inc(st2, 1)
                dve.wait_ge(st2, b + 1)
                if not known(b) or b >= 1:
                    dve.wait_ge(hn_twin, b)
                dve.sem_inc(passed, 1)
                nc.vector.bn_aggr(mv2[:], stat2[:]).then_inc(ag2, 1)

            def lo_of_experts(first, end):
                for e in range(first, end):
                    dve.wait_ge(wgu_hi, e - 1)
                    nc.vector.tensor_tensor(Wgu[:, e, 1], Wgu[:, e, 1].bitcast(F32), Wgu[:, e, 0].bitcast(F32),
                                            ALU.subtract).then_inc(wgu_lo[1], 1)

            def choose(b):
                dve.wait_ge(gates_done, b + 1)
                dve.sem_inc(passed, 1)
                nc.vector.max(top[:], gates[:]).then_inc(top_done, 1)
                dve.wait_ge(top_done, b + 1)
                dve.sem_inc(passed, 1)
                nc.vector.max_index(top_i[:], top[:], gates[:]).then_inc(topi_done, 1)

            def mark(b, slot):
                dve.wait_ge(topi_done, b + 1)
                nc.vector.tensor_copy(top_f[:], top_i[:, 0:2]).then_inc(topf_done, 1)
                nc.vector.tensor_reduce(top_sum[:], top[:, 0:2], AX.X, ALU.add).then_inc(tsum_done, 1)
                dve.wait_ge(topf_done, b + 1)
                nc.vector.tensor_tensor(onehot[:], iota_e[0:LQ, :].unsqueeze(1).to_broadcast([LQ, 2, E]),
                                        top_f[:].unsqueeze(2).to_broadcast([LQ, 2, E]),
                                        ALU.is_equal).then_inc(onehot_done, 1)
                dve.wait_ge(tsum_done, b + 1)
                nc.vector.reciprocal(inv_top[:], top_sum[:]).then_inc(tinv_done, 1)
                dve.wait_ge(onehot_done, b + 1)
                nc.vector.tensor_tensor(chosen[:], onehot[:, 0, :], onehot[:, 1, :], ALU.add).then_inc(chosen_done, 1)
                dve.wait_ge(tinv_done, b + 1)
                nc.vector.tensor_scalar(hn[:, slot, :, C + 1], top[:, 0:2], inv_top[:, 0:1], None, ALU.mult).then_inc(kept, 1)
                if not known(b) or b >= 1:
                    dve.wait_ge(next_dest, b)
                nc.vector.tensor_copy(hn[:, slot, :, C], dest[:]).then_inc(kept, 1)
                nc.vector.tensor_scalar(dest[:], dest[:], float(LQ), None, ALU.add).then_inc(next_dest, 1)

            def assign(b, slot):
                dve.wait_ge(counts_made, b + 1)
                nc.vector.tensor_tensor(bin_at[:], C_ps[0:LQ, 0:E], running[0:LQ, :], ALU.add).then_inc(binat_done, 1)
                dve.wait_ge(binat_done, b + 1)
                nc.vector.tensor_tensor(running[:], C_ps[:, E:2 * E], running[:], ALU.add).then_inc(running_done, 1)
                nc.vector.tensor_tensor(picked[:], onehot[:], bin_at[:].unsqueeze(1).to_broadcast([LQ, 2, E]),
                                        ALU.mult).then_inc(picked_done, 1)
                dve.wait_ge(picked_done, b + 1)
                nc.vector.tensor_reduce(rank2[:], picked[:], AX.X, ALU.add).then_inc(rank_done, 1)
                dve.wait_ge(rank_done, b + 1)
                nc.vector.scalar_tensor_tensor(bin_row[:, slot, :], top_f[:], float(STRIDE), rank2[:],
                                               ALU.mult, ALU.add).then_inc(row_done, 1)

            def pair(i):
                a = Ahead(i) if there(i, NP) else None
                for odd in (0, 1):
                    b = 2 * i + odd
                    for s in range(H):
                        g = H * b + s
                        if s == 2 and there(b - 1, B):
                            normalise(2 * b - 1, 1)
                        if s == 10 and there(b, B):
                            normalise(2 * b, 0)
                        if there(g, B * H):
                            dve.wait_ge(scores_made, g + 1)
                            nc.vector.tensor_reduce(neg_max[:, s % 2:s % 2 + 1], S_ps[s % 2][0:LQ, 0:LKV],
                                                    AX.X, ALU.max, negate=True).then_inc(max_done, 1)
                        if s == 15 and there(b - 1, B):
                            mark(b - 1, 1 - odd)
                        if s == 1 and there(b - 1, B):
                            invert_sums(2 * b - 1, 1)
                        if s == 9 and there(b, B):
                            invert_sums(2 * b, 0)
                        if s == 1 and there(b - 2, B):
                            assign(b - 2, odd)
                        items = a.at(odd, s) if a else []
                        for k in items[:1]:
                            low_part(a, k)
                        if s % 2 == 0 and there(g - 1, B * H):
                            dve.wait_ge(probT_made, g)
                            if not known(g) or g >= 3:
                                dve.wait_ge(pv_made, g - 2)
                            nc.vector.tensor_copy(probT[:, 1, :], PT_ps[1][0:KR, 0:KT * LQ]).then_inc(probT_odd, 1)
                        if s in (3, 11) and there(b - (s == 3), B):
                            half = int(s == 3)
                            dve.wait_ge(OT_hi, 2 * (b - half) + half + 1)
                            nc.vector.tensor_tensor(OT_l[:, 4 * half:4 * half + 4, :].rearrange("p j q -> p (j q)"),
                                                    C_ps[:, 0:4 * LQ],
                                                    OT_h[:, 4 * half:4 * half + 4, :].rearrange("p j q -> p (j q)").bitcast(F32),
                                                    ALU.subtract).then_inc(OT_lo, 1)
                        if known(i) and i == NP and not odd and s == 3:
                            lo_of_experts(2, 4)
                        if s == 5 and there(b - 1, B):
                            residual(i, b - 1, 1 - odd)
                            if known(b) and b == B:
                                lo_of_experts(4, 5)
                        if s == 8 and there(b - 1, B):
                            dve.wait_ge(hnT_made, b)
                            nc.vector.tensor_copy(hnT[:].rearrange("p k q -> p (k q)"), C_ps[:, 0:2 * LQ]).then_inc(hnT_done, 1)
                        if s == 12 and not odd and (not known(i) or i + 1 < NP):
                            norm_x(i + 1)
                        if there(b - 1, B):
                            if s == 13:
                                dve.wait_ge(logits_made, b)
                                nc.vector.tensor_reduce(neg_top[:], C_ps[0:LQ, 0:E], AX.X, ALU.max,
                                                        negate=True).then_inc(top_neg, 1)
                            if s == 14:
                                choose(b - 1)
                        for k in items[1:]:
                            low_part(a, k)

            over_pairs(dve, pair)

            done = [0]

            def step(ins):
                done[0] += 1
                ins.then_inc(plan, 1)
                dve.wait_ge(plan, done[0])

            dve.wait_ge(running_done, B)
            step(nc.vector.tensor_tensor(pad_row[:], iota_p[:], running[:], ALU.add))
            step(nc.vector.tensor_tensor(t_cmp[:], running[:].unsqueeze(2).to_broadcast([P, E, CAP // P]),
                                         iota_tile[:].unsqueeze(1).to_broadcast([P, E, CAP // P]), ALU.is_gt))
            step(nc.vector.tensor_reduce(n_tiles[:], t_cmp[:], AX.X, ALU.add))
            step(nc.vector.tensor_tensor(t_ee[:], n_tiles[:].unsqueeze(1).to_broadcast([P, E, E]), le_mask[:], ALU.mult))
            step(nc.vector.tensor_reduce(cum[:], t_ee[:], AX.X, ALU.add))
            step(nc.vector.tensor_tensor(cum_ex[:], cum[:], n_tiles[:], ALU.subtract))
            step(nc.vector.tensor_tensor(t_te[:], cum[:].unsqueeze(1).to_broadcast([P, NT, E]),
                                         iota_t[:].unsqueeze(2).to_broadcast([P, NT, E]), ALU.is_le))
            step(nc.vector.tensor_reduce(e_of[:], t_te[:], AX.X, ALU.add))
            step(nc.vector.tensor_tensor(t_tc[:], t_te[:], cum[:].unsqueeze(1).to_broadcast([P, NT, E]), ALU.mult))
            step(nc.vector.tensor_reduce(prev[:], t_tc[:], AX.X, ALU.max))
            step(nc.vector.tensor_tensor(within[:], iota_t[:], prev[:], ALU.subtract))
            step(nc.vector.tensor_scalar(within[:], within[:], float(P), None, ALU.mult))
            step(nc.vector.scalar_tensor_tensor(tile_row[:], e_of[:], float(STRIDE), within[:], ALU.mult, ALU.add))
            step(nc.vector.tensor_scalar(tile_expert[:, 1:NT + 1], e_of[:], float(E - 1), None, ALU.min))
            assert done[0] == N_PLAN

            lo_of_experts(6, E)

            def lo_of_rows(t, slot):
                dve.wait_ge(hT_hi, t + 1)
                nc.vector.tensor_tensor(hT_l[:, slot].rearrange("p k n -> p (k n)"), hT_ps[:, 0:2 * P],
                                        hT_h[:, slot].rearrange("p k n -> p (k n)").bitcast(F32),
                                        ALU.subtract).then_inc(hT_lo, 1)

            def keep_dest(t, i, slot):
                if not known(t) or t >= 4:
                    dve.wait_ge(y_store[slot % 2], 16 * i)
                nc.vector.tensor_copy(dest_now[:, slot:slot + 1], h_in[:, slot, C:C + 1])
                nc.vector.tensor_copy(share_now[:, slot:slot + 1], h_in[:, slot, C + 1:C + 2]).then_inc(dest_done, 1)

            lo_of_rows(0, 0)
            keep_dest(0, 0, 0)

            def four_tiles(i):
                for k in range(4):
                    t = 4 * i + k
                    if there(t - 1, NT):
                        dve.wait_ge(hidT_made, t)
                        nc.vector.tensor_copy(hidT[:].rearrange("p j n -> p (j n)"), hidT_ps[:]).then_inc(hidT_done, 1)
                    if there(t + 1, NT):
                        lo_of_rows(t + 1, (k + 1) % 2)
                        keep_dest(t + 1, 2 * i + (k - 3) // 2 + 1, (k + 1) % 4)
                    if there(t, NT):
                        dve.wait_ge(silu_done, t + 1)
                        dve.wait_ge(up_made, t + 1)
                        nc.vector.tensor_tensor(hid[:], up_ps[k % 2][:], silu[:], ALU.mult).then_inc(hid_done, 1)

            over_tiles(dve, four_tiles)

            dve.wait_ge(gx_in[0], 16 * x2_early)
            for n in range(B // G):
                if n == x2_early:
                    dve.wait_ge(gx_in[1], 16 * (B // G - x2_early))
                dve.wait_ge(g_in[n], 32)
                nc.vector.tensor_tensor(g_x[n][:], g_x[n][:], g_rows[:, n, 0], ALU.add).then_inc(gsum_done, 1)
                dve.wait_ge(gsum_done, n + 1)
                nc.vector.tensor_tensor(g_rows[:, n, 0], g_x[n][:], g_rows[:, n, 1], ALU.add).then_inc(gout_done, 1)

        @block.tensor
        def _(pe):
            mm = nc.tensor.matmul

            def split_product(dst, pairs):
                todo = [(w, m) for wh, wl, mh, ml in pairs for w, m in ((wh, mh), (wh, ml), (wl, mh))]
                for n, (w, m) in enumerate(todo):
                    last = mm(dst, w, m, start=n == 0, stop=n == len(todo) - 1)
                return last

            def make(a, k, pair):
                odd, step, kind, arg = a.items[k]
                dst = A_ps[a.bank(k)]
                if not a.first or k >= 2:
                    if k >= 2:
                        if a.items[k - 2][2] == "V":
                            pe.wait_ge(v_done, a.values(k - 2))
                        else:
                            pe.wait_ge(lo_done, a.split(k - 2))
                    else:
                        pe.wait_ge(lo_done, a.split0 - 1 + k)
                slot = 1 - odd
                if kind == "yT":
                    slot = 0 if step < 0 else odd
                    pe.wait_ge(y_in[slot], 32 * (1 if a.first else pair + 2))
                    for t in range(KT):
                        last = nc.tensor.transpose(dst[:, t * KR:t * KR + KR], y_sb[:, slot, t, arg * P:arg * P + P],
                                                   ident[0:KR, 0:KR])
                elif kind == "xT":
                    pe.wait_ge(xn_done, 2 * (0 if a.first else pair + 1) + arg + 1)
                    for t in range(2):
                        last = nc.tensor.transpose(dst[:, t * LQ:t * LQ + LQ], xn[:, arg, t * P:t * P + P],
                                                   ident[0:LQ, 0:LQ])
                elif kind == "K":
                    if arg == 0:
                        pe.wait_ge(lo_done, context_split(a, odd))
                    c = slice(arg * P, arg * P + P)
                    last = product_ctx(dst[:, 0:LKE], c, slot, slice(0, LKE), True)
                elif kind == "q":
                    if arg == 0:
                        pe.wait_ge(lo_done, a.split(a.find(1, "xT", 1)))
                        if a.first:
                            pe.wait_ge(w_lo, 3)
                    c = slice(arg * P, arg * P + P)
                    last = split_product(dst[:, 0:2 * LQ], [(WqH[:, t, c], WqL[:, t, c], xT_h[:, t, :], xT_l[:, t, :])
                                                            for t in range(2)])
                else:
                    half, t = arg
                    if half:
                        slot = odd
                    c = slice(HD + half * 512, HD + half * 512 + 512)
                    last = product_ctx(dst[0:KR, :], c, slot, slice(t * KR, t * KR + KR), False)
                last.then_inc(made, 1)

            def product_ctx(dst, c, slot, rows, weights_stay):
                todo = [(WkvH[:, c], yA_h[:, slot, rows]), (WkvH[:, c], yA_l[:, slot, rows]),
                        (WkvL[:, c], yA_h[:, slot, rows]), (WkvT[:, c], yB[:, slot, rows]),
                        (WkvU[:, c], yB[0:CT, slot, rows])]
                for n, (w, y) in enumerate(todo):
                    last = mm(dst, w if weights_stay else y, y if weights_stay else w,
                              start=n == 0, stop=n == len(todo) - 1)
                return last

            def context_split(a, odd):
                if a.first:
                    return 2
                if odd:
                    return a.split(a.find(0, "yT", 1))
                return a.split_in_pair_before(1, "yT", 1)

            pe.wait_ge(consts, N_CONSTS)
            a = Ahead(None)
            for k in range(len(a.items)):
                if k == 4:
                    pe.wait_ge(w_lo, 2)
                make(a, k, None)

            def scores(a, i, odd, s, g):
                j, r = s // 2, s % 2
                if r == 0:
                    if odd:
                        pe.wait_ge(lo_done, a.split(a.find(0, "K", j)))
                    else:
                        pe.wait_ge(lo_done, a.split_in_pair_before(1, "q", j))
                if not known(g) or g >= 2:
                    pe.wait_ge(exp_done, g - 1)
                rows = slice(r * DK, r * DK + DK)
                q = slice(odd * LQ, odd * LQ + LQ)
                split_product(S_ps[r][0:LQ, 0:LKE], [(q_h[rows, j, q], q_l[rows, j, q], K_h[rows, j, :],
                                                      K_l[rows, j, :])]).then_inc(scores_made, 1)

            def turn_prob(i, odd, s, g):
                k, nth = (s - 1) % 2, 8 * (2 * i + odd) + (s - 1) // 2
                pe.wait_ge(exp_done, g + 1)
                if not known(g) or g >= 2:
                    pe.wait_ge(probT_odd if k else probT_even, nth)
                for t in range(KT):
                    last = nc.tensor.transpose(PT_ps[k][0:KR, t * LQ:t * LQ + LQ],
                                               prob[:, k, t * KR:t * KR + KR], ident[0:LQ, 0:LQ])
                last.then_inc(probT_made, 1)

            def weigh(a, i, odd, s, g):
                k, nth, head = s % 2, 8 * (2 * i + odd) + (s - 2) // 2, (s - 2) % H
                if head % HB == 0:
                    if not known(g) or g >= HB:
                        pe.wait_ge(O_done, 2 * (2 * i + odd) + head // HB)
                    if head:
                        pe.wait_ge(v_done, a.values(a.find(odd, "V", (1, KT - 1))))
                    elif odd:
                        pe.wait_ge(v_done, a.values(a.find(0, "V", (0, KT - 1))))
                    else:
                        pe.wait_ge(v_done, a.values_in_pair_before(1, "V", (0, KT - 1)))
                pe.wait_ge(probT_odd if k else probT_even, nth + 1)
                for t in range(KT):
                    last = mm(O_ps[0:LQ, head % HB * DK:head % HB * DK + DK], probT[:, k, t * LQ:t * LQ + LQ],
                              V[:, t, head * DK:head * DK + DK], start=t == 0, stop=t == KT - 1)
                last.then_inc(pv_made, 1)

            def turn_O(half):
                for j in range(4):
                    last = nc.tensor.transpose(C_ps[:, j * LQ:j * LQ + LQ],
                                               O_sb[:, (4 * half + j) * P:(4 * half + j) * P + P], ident[0:LQ, 0:LQ])
                last.then_inc(OT_made, 1)

            def after_attention(b, s, odd):
                if s == 1 and there(b - 2, B):
                    pe.wait_ge(chosen_done, b - 1)
                    pe.wait_ge(gates_done, b - 1)
                    mm(C_ps[0:LQ, 0:E], before[:], chosen[:], start=True, stop=True)
                    mm(C_ps[:, E:2 * E], ones[:], chosen[:], start=True, stop=True).then_inc(counts_made, 1)
                if s == 3 and there(b - 1, B):
                    pe.wait_ge(O_done, 2 * b)
                    if not known(b) or b >= 2:
                        pe.wait_ge(running_done, b - 1)
                    turn_O(1)
                if s == 5 and there(b - 1, B):
                    pe.wait_ge(OT_lo, 2 * b)
                    if known(b) and b == 1:
                        pe.wait_ge(wp_done, 2)
                    split_product(C_ps[0:LQ, 0:C], [(OT_h[:, j, :], OT_l[:, j, :], WpH[:, j, :], WpL[:, j, :])
                                                    for j in range(NJ)]).then_inc(proj_made, 1)
                if s == 8 and there(b - 1, B):
                    pe.wait_ge(x2_done, b)
                    pe.wait_ge(hn_done, b)
                    for t in range(2):
                        last = nc.tensor.transpose(C_ps[:, t * LQ:t * LQ + LQ], hn[:, 1 - odd, 0, t * P:t * P + P],
                                                   ident[0:LQ, 0:LQ])
                    last.then_inc(hnT_made, 1)
                if s == 11 and there(b, B):
                    pe.wait_ge(O_done, 2 * b + 1)
                    if not known(b) or b >= 1:
                        pe.wait_ge(hnT_done, b)
                    turn_O(0)
                if s == 13 and there(b - 1, B):
                    pe.wait_ge(hnT_done, b)
                    if there(b, B):
                        pe.wait_ge(OT_lo, 2 * b + 1)
                    if known(b) and b == 1:
                        pe.wait_ge(small_in, 32)
                    for t in range(2):
                        last = mm(C_ps[0:LQ, 0:E], hnT[:, t, :], gw[:, t, :], start=t == 0, stop=t == 1)
                    last.then_inc(logits_made, 1)

            def pair(i):
                a = Ahead(i) if there(i, NP) else None
                for odd in (0, 1):
                    b = 2 * i + odd
                    for s in range(H):
                        g = H * b + s
                        if there(g, B * H):
                            scores(a, i, odd, s, g)
                        items = a.at(odd, s) if a else []
                        for k in items[:1]:
                            make(a, k, i)
                        if there(g - 1, B * H):
                            turn_prob(i, odd, s, g - 1)
                        after_attention(b, s, odd)
                        if there(g - 2, B * H):
                            weigh(a, i, odd, s, g - 2)
                        for k in items[1:]:
                            make(a, k, i)

            over_pairs(pe, pair)

            pe.wait_ge(plan, N_PLAN)
            pe.wait_ge(running_done, B)

            def turn_rows(i, t, slot):
                pe.wait_ge(h_in_ld[slot], 16 * (i + 1))
                for j in range(2):
                    last = nc.tensor.transpose(hT_ps[:, j * P:j * P + P], h_in[:, slot, j * P:j * P + P], ident[:])
                last.then_inc(hT_made, 1)

            def experts_from(i, first, n):
                c = 4 * i + first + 1
                return nc.values_load_multi_w_load_instructions(
                    tile_expert[0:1, c:c + n] if known(i) else tile_expert[0:1, bass.ds(c, n)],
                    engines=(mybir.EngineType.PE,), min_val=0, max_val=E - 1)[1]

            def hidden(dst, e, slot, half):
                c = slice(half * FF, half * FF + FF)
                return split_product(dst, [(hT_h[:, slot, j, :], hT_l[:, slot, j, :], Wgu[:, e, 0, j, c], Wgu[:, e, 1, j, c])
                                           for j in range(2)])

            def gate(t, e, slot):
                pe.wait_ge(hT_lo, t + 1)
                if not known(t) or t >= 2:
                    pe.wait_ge(silu_done, t - 1)
                hidden(gate_ps[slot][:], e, slot, 0).then_inc(gate_made, 1)

            turn_rows(0, 0, 0)
            for k, lo_parts in enumerate((3, E - 3)):
                pe.wait_ge(wgu_lo[k], lo_parts)
            gate(0, experts_from(0, 0, 1)[0], 0)

            def four_tiles(i):
                experts = experts_from(i, -1, 4)
                for k in range(4):
                    t = 4 * i + k
                    if k == 1:
                        experts += experts_from(i, 3, 2)
                    if there(t - 1, NT):
                        pe.wait_ge(hid_done, t)
                        if not known(t) or t >= 2:
                            pe.wait_ge(hidT_done, t - 1)
                        for j in range(FJ):
                            last = nc.tensor.transpose(hidT_ps[:, j * P:j * P + P], hid[:, j * P:j * P + P], ident[:])
                        last.then_inc(hidT_made, 1)
                    if there(t + 1, NT):
                        turn_rows(i if k < 3 else i + 1, t + 1, (k + 1) % 4)
                    if there(t, NT):
                        if not known(t) or t >= 2:
                            pe.wait_ge(hid_done, t - 1)
                        hidden(up_ps[k % 2][:], experts[k + 1], k % 2, 1).then_inc(up_made, 1)
                    if there(t - 1, NT):
                        pe.wait_ge(hidT_done, t)
                        if known(t) and t == 1:
                            pe.wait_ge(wd_early, 16)
                            pe.wait_ge(wd_in, 16)
                        if not known(t) or t >= 3:
                            pe.wait_ge(y_done, t - 2)
                        for j in range(FJ):
                            last = mm(down_ps[(k + 1) % 2][:, 0:C], hidT[:, j, :], Wd[:, experts[k], j, :],
                                      start=j == 0, stop=j == FJ - 1)
                        last.then_inc(down_made, 1)
                    if there(t + 1, NT):
                        gate(t + 1, experts[k + 2], (k + 1) % 2)

            over_tiles(pe, four_tiles)


_INS = ["x", "ctx_768", "L0_xattn_Wq", "L0_xattn_Wkv", "L0_xattn_Wproj", "L0_xattn_bproj",
        "L0_ffn_gate_w", "L0_ffn_gate_up_w", "L0_ffn_down_w"]


def kernel(**inputs):
    from concourse import bacc
    from concourse.bass_utils import run_bass_kernel_spmd

    nc = bacc.Bacc("TRN2", target_bir_lowering=False, num_devices=1)
    arrays, args = {}, []
    for name in _INS:
        a = np.ascontiguousarray(inputs[name])
        arrays[f"in_{name}"] = a
        args.append(nc.dram_tensor(f"in_{name}", a.shape, mybir.dt.from_np(a.dtype), kind="ExternalInput").ap())
    out = nc.dram_tensor("out", (B, LQ, C), F32, kind="ExternalOutput").ap()
    attention_and_experts(nc, *args, out)
    r = run_bass_kernel_spmd(nc, [arrays], core_ids=[0])
    return r.results[0]["out"]
```
